# Optimizing a Trainium2 kernel written in Bass

```python
import numpy as np
import jax
import jax.numpy as jnp

def _softmax(x, axis=-1):
    return jax.nn.softmax(x, axis=axis)

def _gelu(x):
    return jax.nn.gelu(x, approximate=True)

def _silu(x):
    return jax.nn.silu(x)

def _sigmoid(x):
    return jax.nn.sigmoid(x)

def _layernorm(x, axis=-1, eps=1e-05):
    m = jnp.mean(x, axis=axis, keepdims=True)
    v = jnp.var(x, axis=axis, keepdims=True)
    return (x - m) / jnp.sqrt(v + eps)

def _scatter_add(tgt, idx, src, axis=0):
    return tgt.at[idx].add(src)

def _segment_sum(src, seg, n):
    return jax.ops.segment_sum(src, seg, n)
kernel_name = 'mk_flamingo_gated_d2_seqx_r4_f915b0'

def setup_inputs(seed: int=0):
    np.random.seed(seed)
    _w = jnp.asarray

    def _rec_inputs():
        import jax
        import jax.numpy as jnp
        _rk = jax.random.key(seed)
        x = -0.0002928 + 1 * jax.random.normal(jax.random.fold_in(_rk, 1), (2, 1024, 256), jnp.float32)
        _lenS = 1024 - jax.random.randint(jax.random.fold_in(_rk, 7), (2,), 0, max(1, 1024 // 4) + 1, jnp.int32)
        _lenS2 = 77 - jax.random.randint(jax.random.fold_in(_rk, 8), (2,), 0, max(1, 77 // 4) + 1, jnp.int32)
        _ctx_1024P = jax.random.normal(jax.random.fold_in(_rk, 11), (2, 16, 256), jnp.float32)
        _ctx_1024c = jax.random.dirichlet(jax.random.fold_in(_rk, 511), 0.3 * jnp.ones((16,), jnp.float32), (2, 77))
        _ctx_1024t = jnp.einsum('bsk,bkd->bsd', _ctx_1024c, _ctx_1024P)
        _ctx_1024t = _ctx_1024t * jax.lax.rsqrt(jnp.mean(jnp.square(_ctx_1024t)) + 1e-12) * 0.953939
        ctx_1024 = 2.81802e-05 + 1.00001 * (_ctx_1024t + 0.3 * jax.random.normal(jax.random.fold_in(_rk, 611), (2, 77, 256), jnp.float32))
        _validS = jnp.arange(1024)[None, :] < _lenS[:, None]
        _validS2 = jnp.arange(77)[None, :] < _lenS2[:, None]
        _causal = jnp.tril(jnp.ones((1024, 1024), dtype=bool))
        mask_BxS2_bk0 = jnp.logical_not(jnp.broadcast_to(_validS2[:, :], (2, 77)))
        mask_1xSxS2_ff0 = jnp.where(jnp.ones((1, 1024, 77), dtype=bool), 0.0, -1000000000.0).astype(jnp.float32)
        _g = jax.random.normal(jax.random.fold_in(_rk, 9001), (2, 2), jnp.float32)
        _g = jnp.sign(_g) * jnp.maximum(jnp.abs(_g), 1.0) + (_g == 0) * 1.0
        g_xattn = _g[0]
        g_ffn = _g[1]
        return (x, ctx_1024, mask_BxS2_bk0, mask_1xSxS2_ff0, g_xattn, g_ffn)
    x, ctx_1024, mask_BxS2_bk0, mask_1xSxS2_ff0, g_xattn, g_ffn = _rec_inputs()

    def _L0_xattn_setup():
        import jax, jax.numpy as jnp
        import numpy as np
        NUM_HEADS, NUM_KV, HEAD_DIM, WIDTH = (4, 1, 64, 256)
        MASK_FILL = -2.3819763e+38

        def _apply_rope(x, positions, max_wavelength=10000.0):
            d = x.shape[-1]
            freq_exp = 2.0 / d * jnp.arange(d // 2, dtype=jnp.float32)
            timescale = max_wavelength ** freq_exp
            radians = positions[..., None].astype(jnp.float32) / timescale
            radians = radians[..., None, :]
            sin, cos = (jnp.sin(radians), jnp.cos(radians))
            x1, x2 = jnp.split(x, 2, axis=-1)
            out = jnp.concatenate([x1 * cos - x2 * sin, x2 * cos + x1 * sin], axis=-1)
            return out.astype(x.dtype)

        def _rmsnorm(x, scale):
            var = jnp.mean(jnp.square(x.astype(jnp.float32)), axis=-1, keepdims=True)
            normed = x * jax.lax.rsqrt(var + 1e-06)
            return (normed * (1 + scale)).astype(x.dtype)
        key = jax.random.key(seed)
        ks = jax.random.split(key, 7)
        B, T, S = (8, 128, 512)
        return {'x': jax.random.normal(ks[0], (B, T, WIDTH), jnp.float32), 'mem_seq': jax.random.normal(ks[1], (B, S, WIDTH), jnp.float32), 'mem_mask': jax.random.randint(ks[2], (B, S), 0, 2).astype(bool), 'rms_scale': jax.random.normal(ks[3], (WIDTH,), jnp.float32) * 0.02, 'q_w': jax.random.normal(ks[4], (NUM_HEADS, WIDTH, HEAD_DIM), jnp.float32) / np.sqrt(WIDTH), 'kv_w': jax.random.normal(ks[5], (2, NUM_KV, WIDTH, HEAD_DIM), jnp.float32) / np.sqrt(WIDTH), 'out_w': jax.random.normal(ks[6], (NUM_HEADS, HEAD_DIM, WIDTH), jnp.float32) / np.sqrt(NUM_HEADS * HEAD_DIM)}
    _L0_xattn_all = _L0_xattn_setup()
    _L0_xattn_in = {k: v for k, v in _L0_xattn_all.items() if k in ('rms_scale', 'q_w', 'kv_w', 'out_w')}
    del _L0_xattn_all

    def _L0_ffn_setup():
        import jax, jax.numpy as jnp
        import numpy as np
        N_EMBD = 256
        N_STATE = 1024
        key = jax.random.key(seed)
        k_x, k_w1, k_b1, k_w2, k_b2 = jax.random.split(key, 5)
        x = jax.random.normal(k_x, (4, 512, N_EMBD), dtype=jnp.float32)
        w1 = jax.random.normal(k_w1, (N_EMBD, N_STATE), dtype=jnp.float32) * (1.0 / np.sqrt(N_EMBD))
        b1 = jax.random.normal(k_b1, (N_STATE,), dtype=jnp.float32) * 0.02
        w2 = jax.random.normal(k_w2, (N_STATE, N_EMBD), dtype=jnp.float32) * (1.0 / np.sqrt(N_STATE))
        b2 = jax.random.normal(k_b2, (N_EMBD,), dtype=jnp.float32) * 0.02
        return {'x': x, 'w1': w1, 'b1': b1, 'w2': w2, 'b2': b2}
    _L0_ffn_all = _L0_ffn_setup()
    _L0_ffn_in = {k: v for k, v in _L0_ffn_all.items() if k in ('w1', 'b1', 'w2', 'b2')}
    del _L0_ffn_all

    def _L1_xattn_setup():
        import jax, jax.numpy as jnp
        import numpy as np
        B, S, D_IN, D_MODEL = (4, 512, 256, 256)
        key = jax.random.key(seed)
        ks = jax.random.split(key, 8)
        glorot = np.sqrt(6.0 / (D_IN + D_MODEL))
        inp = {'q': jax.random.normal(ks[0], (B, S, D_IN), dtype=jnp.float32), 'k': jax.random.normal(ks[1], (B, S, D_IN), dtype=jnp.float32), 'v': jax.random.normal(ks[2], (B, S, D_IN), dtype=jnp.float32), 'mask': jnp.zeros((1, S, S), dtype=jnp.float32), 'kernel_q': jax.random.uniform(ks[3], (1, 1, D_IN, D_MODEL), jnp.float32, -glorot, glorot), 'kernel_k': jax.random.uniform(ks[4], (1, 1, D_IN, D_MODEL), jnp.float32, -glorot, glorot), 'kernel_v': jax.random.uniform(ks[5], (1, 1, D_IN, D_MODEL), jnp.float32, -glorot, glorot), 'bias_q': 0.05 * jax.random.normal(ks[6], (D_MODEL,), dtype=jnp.float32), 'bias_k': 0.05 * jax.random.normal(ks[7], (D_MODEL,), dtype=jnp.float32), 'bias_v': 0.05 * jax.random.normal(jax.random.fold_in(key, 7), (D_MODEL,), dtype=jnp.float32)}
        return inp
    _L1_xattn_all = _L1_xattn_setup()
    _L1_xattn_in = {k: v for k, v in _L1_xattn_all.items() if k in ('kernel_q', 'kernel_k', 'kernel_v', 'bias_q', 'bias_k', 'bias_v')}
    del _L1_xattn_all

    def _L1_ffn_setup():
        import jax, jax.numpy as jnp
        import numpy as np
        D_MODEL, D_FF, NUM_EXPERTS, RANK, TOP_K = (256, 1024, 8, 16, 2)
        B, S = (8, 512)

        def _expert_ffn(h, wi_w, wo_w, A, Bm):
            inter = jnp.einsum('bsd,fd->bsf', h, wi_w)
            lora = jnp.einsum('bsr,fr->bsf', jnp.einsum('bsd,rd->bsr', h, A), Bm)
            inter = jax.nn.relu(inter + lora)
            return jnp.einsum('bsf,df->bsd', inter, wo_w)
        key = jax.random.key(seed)
        ks = jax.random.split(key, 8)
        hidden_states = jax.random.normal(ks[0], (B, S, D_MODEL), dtype=jnp.float32)
        wi_w = jax.random.normal(ks[1], (D_FF, D_MODEL), dtype=jnp.float32) * (1.0 / np.sqrt(D_MODEL))
        wo_w = jax.random.normal(ks[2], (D_MODEL, D_FF), dtype=jnp.float32) * (1.0 / np.sqrt(D_FF))
        lora_As = jax.random.uniform(ks[3], (NUM_EXPERTS, RANK, D_MODEL), dtype=jnp.float32, minval=-1.0, maxval=1.0) / np.sqrt(D_MODEL)
        lora_Bs = jax.random.normal(ks[4], (NUM_EXPERTS, D_FF, RANK), dtype=jnp.float32) * 0.02
        top_k_indices = jnp.arange(TOP_K, dtype=jnp.int32)
        top_k_values = jax.random.uniform(ks[5], (TOP_K,), dtype=jnp.float32)
        return {'hidden_states': hidden_states, 'wi_w': wi_w, 'wo_w': wo_w, 'lora_As': lora_As, 'lora_Bs': lora_Bs, 'top_k_indices': top_k_indices, 'top_k_values': top_k_values}
    _L1_ffn_all = _L1_ffn_setup()
    _L1_ffn_in = {k: v for k, v in _L1_ffn_all.items() if k in ('wi_w', 'wo_w', 'lora_As', 'lora_Bs', 'top_k_indices', 'top_k_values')}
    del _L1_ffn_all
    return {'x': x, 'ctx_1024': ctx_1024, 'mask_BxS2_bk0': mask_BxS2_bk0, 'mask_1xSxS2_ff0': mask_1xSxS2_ff0, 'g_xattn': g_xattn, 'g_ffn': g_ffn, 'L0_xattn_rms_scale': _L0_xattn_in['rms_scale'], 'L0_xattn_q_w': _L0_xattn_in['q_w'], 'L0_xattn_kv_w': _L0_xattn_in['kv_w'], 'L0_xattn_out_w': _L0_xattn_in['out_w'], 'L0_ffn_w1': _L0_ffn_in['w1'], 'L0_ffn_b1': _L0_ffn_in['b1'], 'L0_ffn_w2': _L0_ffn_in['w2'], 'L0_ffn_b2': _L0_ffn_in['b2'], 'L1_xattn_kernel_q': _L1_xattn_in['kernel_q'], 'L1_xattn_kernel_k': _L1_xattn_in['kernel_k'], 'L1_xattn_kernel_v': _L1_xattn_in['kernel_v'], 'L1_xattn_bias_q': _L1_xattn_in['bias_q'], 'L1_xattn_bias_k': _L1_xattn_in['bias_k'], 'L1_xattn_bias_v': _L1_xattn_in['bias_v'], 'L1_ffn_wi_w': _L1_ffn_in['wi_w'], 'L1_ffn_wo_w': _L1_ffn_in['wo_w'], 'L1_ffn_lora_As': _L1_ffn_in['lora_As'], 'L1_ffn_lora_Bs': _L1_ffn_in['lora_Bs'], 'L1_ffn_top_k_indices': _L1_ffn_in['top_k_indices'], 'L1_ffn_top_k_values': _L1_ffn_in['top_k_values']}

def reference(x, ctx_1024, mask_BxS2_bk0, mask_1xSxS2_ff0, g_xattn, g_ffn, L0_xattn_rms_scale, L0_xattn_q_w, L0_xattn_kv_w, L0_xattn_out_w, L0_ffn_w1, L0_ffn_b1, L0_ffn_w2, L0_ffn_b2, L1_xattn_kernel_q, L1_xattn_kernel_k, L1_xattn_kernel_v, L1_xattn_bias_q, L1_xattn_bias_k, L1_xattn_bias_v, L1_ffn_wi_w, L1_ffn_wo_w, L1_ffn_lora_As, L1_ffn_lora_Bs, L1_ffn_top_k_indices, L1_ffn_top_k_values):
    import jax
    import jax.numpy as jnp

    def _L0_xattn_ref(x, mem_seq, mem_mask, rms_scale, q_w, kv_w, out_w):
        import jax, jax.numpy as jnp
        import numpy as np
        NUM_HEADS, NUM_KV, HEAD_DIM, WIDTH = (4, 1, 64, 256)
        MASK_FILL = -2.3819763e+38

        def _apply_rope(x, positions, max_wavelength=10000.0):
            d = x.shape[-1]
            freq_exp = 2.0 / d * jnp.arange(d // 2, dtype=jnp.float32)
            timescale = max_wavelength ** freq_exp
            radians = positions[..., None].astype(jnp.float32) / timescale
            radians = radians[..., None, :]
            sin, cos = (jnp.sin(radians), jnp.cos(radians))
            x1, x2 = jnp.split(x, 2, axis=-1)
            out = jnp.concatenate([x1 * cos - x2 * sin, x2 * cos + x1 * sin], axis=-1)
            return out.astype(x.dtype)

        def _rmsnorm(x, scale):
            var = jnp.mean(jnp.square(x.astype(jnp.float32)), axis=-1, keepdims=True)
            normed = x * jax.lax.rsqrt(var + 1e-06)
            return (normed * (1 + scale)).astype(x.dtype)
        B, S, _ = mem_seq.shape
        T = x.shape[1]
        G = NUM_HEADS // NUM_KV
        xn = _rmsnorm(x, rms_scale)
        mn = _rmsnorm(mem_seq, rms_scale)
        q = jnp.einsum('BTD,NDH->BTNH', xn, q_w)
        kv = jnp.einsum('BSD,cKDH->cBSKH', mn, kv_w)
        k, v = (kv[0], kv[1])
        q_pos = jnp.broadcast_to(jnp.arange(S, T + S), (B, T))
        k_pos = jnp.broadcast_to(jnp.arange(S), (B, S))
        q = _apply_rope(q, q_pos) * HEAD_DIM ** (-0.5)
        k = _apply_rope(k, k_pos)
        q = q.reshape(B, T, NUM_KV, G, HEAD_DIM)
        logits = jnp.einsum('BTKGH,BSKH->BKGTS', q, k, preferred_element_type=jnp.float32)
        masked = jnp.where(mem_mask[:, None, None, None, :], logits, MASK_FILL)
        probs = jax.nn.softmax(masked, axis=-1).astype(x.dtype)
        enc = jnp.einsum('BKGTS,BSKH->BTKGH', probs, v).reshape(B, T, NUM_HEADS, HEAD_DIM)
        return jnp.einsum('BTNH,NHD->BTD', enc, out_w)

    def _L0_ffn_ref(x, w1, b1, w2, b2):
        import jax, jax.numpy as jnp
        import numpy as np
        N_EMBD = 256
        N_STATE = 1024
        h = jax.nn.gelu(jnp.einsum('bse,eh->bsh', x, w1) + b1, approximate=False)
        return jnp.einsum('bsh,he->bse', h, w2) + b2

    def _L1_xattn_ref(q, k, v, mask, kernel_q, kernel_k, kernel_v, bias_q, bias_k, bias_v):
        import jax, jax.numpy as jnp
        import numpy as np
        B, S, D_IN, D_MODEL = (4, 512, 256, 256)
        Wq, Wk, Wv = (kernel_q[0, 0], kernel_k[0, 0], kernel_v[0, 0])
        qp = jax.nn.relu(jnp.einsum('bsd,de->bse', q, Wq) + bias_q)
        kp = jax.nn.relu(jnp.einsum('bsd,de->bse', k, Wk) + bias_k)
        vp = jax.nn.relu(jnp.einsum('bsd,de->bse', v, Wv) + bias_v)
        scores = jax.nn.relu(jnp.einsum('bqe,bke->bqk', qp, kp))
        dk = jnp.asarray(kp.shape[-1], dtype=scores.dtype)
        logits = scores / jnp.sqrt(dk) + mask
        out = jax.nn.relu(jnp.einsum('bqk,bke->bqe', logits, vp))
        return out

    def _L1_ffn_ref(hidden_states, wi_w, wo_w, lora_As, lora_Bs, top_k_indices, top_k_values):
        import jax, jax.numpy as jnp
        import numpy as np
        D_MODEL, D_FF, NUM_EXPERTS, RANK, TOP_K = (256, 1024, 8, 16, 2)
        B, S = (8, 512)

        def _expert_ffn(h, wi_w, wo_w, A, Bm):
            inter = jnp.einsum('bsd,fd->bsf', h, wi_w)
            lora = jnp.einsum('bsr,fr->bsf', jnp.einsum('bsd,rd->bsr', h, A), Bm)
            inter = jax.nn.relu(inter + lora)
            return jnp.einsum('bsf,df->bsd', inter, wo_w)
        out = jnp.zeros_like(hidden_states)
        for k in range(top_k_values.shape[0]):
            A = jnp.take(lora_As, top_k_indices[k], axis=0)
            Bm = jnp.take(lora_Bs, top_k_indices[k], axis=0)
            out = out + top_k_values[k] * _expert_ffn(hidden_states, wi_w, wo_w, A, Bm)
        return out
    x = x + jnp.tanh(g_xattn[0]) * _L0_xattn_ref(_layernorm(x, axis=-1), ctx_1024, mask_BxS2_bk0, L0_xattn_rms_scale, L0_xattn_q_w, L0_xattn_kv_w, L0_xattn_out_w)
    x = x + jnp.tanh(g_ffn[0]) * _L0_ffn_ref(_layernorm(x, axis=-1), L0_ffn_w1, L0_ffn_b1, L0_ffn_w2, L0_ffn_b2)
    x = x + jnp.tanh(g_xattn[1]) * _L1_xattn_ref(_layernorm(x, axis=-1), ctx_1024, ctx_1024, mask_1xSxS2_ff0, L1_xattn_kernel_q, L1_xattn_kernel_k, L1_xattn_kernel_v, L1_xattn_bias_q, L1_xattn_bias_k, L1_xattn_bias_v)
    x = x + jnp.tanh(g_ffn[1]) * _L1_ffn_ref(_layernorm(x, axis=-1), L1_ffn_wi_w, L1_ffn_wo_w, L1_ffn_lora_As, L1_ffn_lora_Bs, L1_ffn_top_k_indices, L1_ffn_top_k_values)
    return x

_drawn_inputs = setup_inputs


def setup_inputs(seed=0):
    import zlib

    import numpy as np

    out = dict(_drawn_inputs(seed))
    spreads = {'g_ffn': (-1.0, 0.6)}
    factors = {'L0_xattn_rms_scale': 64.0,
     'L0_ffn_b1': 64.0,
     'L0_ffn_b2': 61.748,
     'L1_xattn_bias_q': 23.277,
     'L1_xattn_bias_k': 21.002,
     'L1_ffn_wi_w': 6.708,
     'L1_ffn_wo_w': 5.32,
     'L1_ffn_lora_As': 8.0,
     'L1_ffn_lora_Bs': 8.0,
     'L1_ffn_top_k_values': 8.0,
     'L0_xattn_q_w': 4.07,
     'L0_ffn_w1': 2.961}
    for name, (base, spread) in spreads.items():
        noise = np.random.default_rng([zlib.crc32(name.encode()), seed]).standard_normal(out[name].shape)
        drawn = base * np.exp(spread * noise) if base else spread * noise
        out[name] = jnp.asarray(drawn.astype(out[name].dtype))
    for name, factor in factors.items():
        out[name] = (out[name] * factor).astype(out[name].dtype)
    return out
```

```python
from contextlib import ExitStack

import numpy as np

import concourse.bass as bass
from concourse import mybir

F32 = mybir.dt.float32
F32R = mybir.dt.float32r
BF16 = mybir.dt.bfloat16
I32 = mybir.dt.int32
U8 = mybir.dt.uint8
ALU = mybir.AluOpType
ACT = mybir.ActivationFunctionType
AX_X = mybir.AxisListType.X

P = 128
BATCH, SEQ, D = 2, 1024, 256
CTX = 77
HEADS, HEAD = 4, 64
PAIR = 2 * CTX
LOGITS = HEADS * CTX
PCH = -(-LOGITS // 3)
PPAD = 3 * PCH
FF = 1024
FCH = FF // P
DCH = D // P
GROUP = 512
TILES = GROUP // P
A, B = 0, 1
EXPERTS, RANK = 8, 16
LORA = 3 * 2 * RANK
RING = 3
MASK_FILL = -2.3819763e+38
LN_EPS, RMS_EPS = 1e-5, 1e-6

C_ID, C_RMS, C_B1, C_GATE, C_BQ, C_BK, C_V, C_LANE = 0, 128, 130, 138, 142, 144, 146, 148
C_B2 = C_LANE + LORA
C_BV = C_B2 + D
C_FILL = C_BV + D
C_END = C_FILL + 2
PREP = {"wq0": 5, "bk16": 8, "gb2": 9, "pick": 16, "wq1": 18, "la": 20, "lb0": 24, "lbd": 28}


def attention0(g):
    return [[("norm", 0, g)], [("lnT", 0, g)], [("q", g)], [("qT", g)], [("lg", g)], [("soft", g)],
            [("pT", g)], [("pv", g)], [("res0", g), ("norm", 1, g)], [("lnT", 1, g)]]


def attention1(g):
    return [[("norm", 2, g)], [("lnT", 2, g)], [("qp", g)], [("sc", g)], [("out", g)], [("res1", g)],
            [("norm", 3, g)], [("lnT", 3, g)], [("u", g)], []]


def ffn0(g):
    steps = []
    for s in range(FCH + 2):
        step = []
        if s < FCH:
            step += [("up0", g, s)]
        if s >= 2:
            step += [("down", 0, g, s - 2)]
        steps.append(step)
    return steps


def ffn1(g):
    steps = []
    for s in range(FCH + 2):
        step = []
        if s < FCH:
            step += [("base1", g, s)]
        if 1 <= s <= FCH:
            step += [("delta1", g, s - 1)]
        if s >= 2:
            step += [("down", 1, g, s - 2)]
        steps.append(step)
    return steps


def beside(main, other):
    out = []
    for m, o in zip(main, other):
        out += m + o
    return out


def flat(steps):
    return [s for step in steps for s in step]


def plan():
    a0 = attention0(A)
    ctx = {0: [("kv",)], 1: [("kvT",)], 3: [("vo",)], 5: [("kp",)], 6: [("vp",)]}
    order = []
    for n, step in enumerate(a0):
        order += step + ctx.get(n, [])
    order += beside(ffn0(A), attention0(B)) + [("resf", 0, A)]
    order += beside(ffn0(B), attention1(A)) + [("resf", 0, B)]
    order += beside(ffn1(A), attention1(B)) + [("resf", 1, A)]
    order += flat(ffn1(B)) + [("resf", 1, B)]
    return order


PLAN = plan()

TILES_OF = {
    "lnT": lambda l, g: [("lnT", l, g, c) for c in range(DCH)],
    "q": lambda g: [("q", g, h) for h in range(2)],
    "qT": lambda g: [("qT", g, p) for p in range(2)],
    "lg": lambda g: [("lg", g, t) for t in range(TILES)],
    "pT": lambda g: [("pT", g, k) for k in range(3)],
    "qp": lambda g: [("qp", g, c) for c in range(DCH)],
    "sc": lambda g: [("sc", g)],
    "u": lambda g: [("u", g)],
    "kv": lambda: [("kv",)],
    "kvT": lambda: [("kvT",)],
    "vo": lambda: [("vo", 0), ("vo", 1)],
    "kp": lambda: [("kp",)],
    "vp": lambda: [("vp",)],
}
SIDE = [t for s in PLAN if s[0] in TILES_OF for t in TILES_OF[s[0]](*s[1:])]
assert len(SIDE) % 2 == 0
CHUNKS = [(l, g, c) for l in range(2) for g in (A, B) for c in range(FCH)]


class Signal:

    def __init__(self, sem, keys):
        self.sem, self.keys = sem, list(keys)
        self.number = {k: n for n, k in enumerate(self.keys)}

    def at(self, i, *key):
        return i * len(self.keys) + (self.number[key] + 1)


def gated_flamingo(nc, t_in, x_out):
    with ExitStack() as ctx:
        def sb(name, shape, dt=F32):
            return ctx.enter_context(nc.sbuf_tensor(name, shape, dt))

        def sem(name):
            return ctx.enter_context(nc.semaphore(name))

        def signal(name, keys):
            return Signal(sem(name), keys)

        small = sb("small", [P, C_END])
        rope_q = sb("rope_q", [P, SEQ // P, 2, HEAD])
        rope_k = sb("rope_k", [CTX, 2, 2 * HEAD])
        stage = sb("stage", [P, 2, FF])
        wq0_h, wq0_l = sb("wq0_h", [P, DCH, D], F32R), sb("wq0_l", [P, DCH, D], F32R)
        wq1_h, wq1_l = sb("wq1_h", [P, DCH, D], F32R), sb("wq1_l", [P, DCH, D], F32R)
        w1_h, w1_l = sb("w1_h", [P, DCH, FF], F32R), sb("w1_l", [P, DCH, FF], F32R)
        w2_h, w2_l = sb("w2_h", [P, FCH, D], F32R), sb("w2_l", [P, FCH, D], F32R)
        wi_h, wi_l = sb("wi_h", [P, DCH, FF], F32R), sb("wi_l", [P, DCH, FF], F32R)
        wo_h, wo_l = sb("wo_h", [P, FCH, D], F32R), sb("wo_l", [P, FCH, D], F32R)
        wkv0 = sb("wkv0", [P, DCH, 4 * HEAD])
        wk1 = sb("wk1", [P, DCH, D])
        wv1 = sb("wv1", [P, DCH, D])
        out_w = sb("out_w", [P, 2, D])
        mask1 = sb("mask1", [CTX, SEQ])
        la_h, la_l = sb("la_h", [P, DCH, LORA], F32R), sb("la_l", [P, DCH, LORA], F32R)
        lb0 = sb("lb0", [LORA, FF], F32R)
        lbd = sb("lbd", [LORA, FF], F32R)
        rms1 = sb("rms1", [P, DCH])
        gate = sb("gate", [P, 4])
        gb2 = sb("gb2", [P, D])
        bk16 = sb("bk16", [P, DCH])
        minus_half = sb("minus_half", [P, TILES])
        topk = sb("topk", [P, 2], I32)
        topk16 = sb("topk16", [P, 2])
        pick = sb("pick", [P, 3, LORA])
        ones3 = sb("ones3", [3, P], BF16)

        ctx_rows = sb("ctx_rows", [CTX, D])
        ctx_T = sb("ctx_T", [P, DCH, CTX])
        mask0 = sb("mask0", [3, CTX], U8)
        mask_row = sb("mask_row", [3, LOGITS], BF16)
        c_st, c_mv, c_sq, c_rms = sb("c_st", [CTX, 6]), sb("c_mv", [CTX, 2]), sb("c_sq", [CTX, 2]), sb("c_rms", [CTX, 1])
        kv = sb("kv", [CTX, 4 * HEAD])
        k_cos, k_sin = sb("k_cos", [CTX, 2 * HEAD]), sb("k_sin", [CTX, 2 * HEAD])
        kb_h, kb_l = sb("kb_h", [P, PAIR], F32R), sb("kb_l", [P, PAIR], F32R)
        v_pad = sb("v_pad", [P, 2, PPAD])
        vo_h, vo_l = sb("vo_h", [PCH, 3, D], F32R), sb("vo_l", [PCH, 3, D], F32R)
        kp_f = sb("kp_f", [P, DCH, CTX])
        kp_h, kp_l = sb("kp_h", [P, DCH, CTX], F32R), sb("kp_l", [P, DCH, CTX], F32R)
        vp_f = sb("vp_f", [CTX, D])
        vp_h, vp_l = sb("vp_h", [CTX, D], F32R), sb("vp_l", [CTX, D], F32R)

        x = sb("x", [P, 2, TILES, D])
        xn = sb("xn", [P, TILES, D])
        T_h = [sb(f"T_h{g}", [P, DCH, GROUP], F32R) for g in (A, B)]
        T_l = [sb(f"T_l{g}", [P, DCH, GROUP], F32R) for g in (A, B)]
        T3_h, T3_l = sb("T3_h", [P, GROUP], F32R), sb("T3_l", [P, GROUP], F32R)

        def pT_h(g, k):
            return T_h[g][0:PCH, k, :] if k < DCH else T3_h[0:PCH, :]

        def pT_l(g, k):
            return T_l[g][0:PCH, k, :] if k < DCH else T3_l[0:PCH, :]

        q_h, q_l = sb("q_h", [P, 2, GROUP], F32R), sb("q_l", [P, 2, GROUP], F32R)
        probs = sb("probs", [P, TILES, PPAD])
        wide = sb("wide", [P, 2, GROUP])
        st, mv = sb("st", [P, TILES, 6]), sb("mv", [P, TILES, 2])
        var, rstd = sb("var", [P, TILES]), sb("rstd", [P, TILES])
        peak = sb("peak", [P, TILES, HEADS])
        total, inv = sb("total", [P, TILES, HEADS]), sb("inv", [P, TILES, HEADS])
        u3 = [sb(f"u3_{g}", [LORA, GROUP], F32R) for g in (A, B)]
        hid = sb("hid", [P, RING, GROUP])
        hid_h, hid_l = sb("hid_h", [P, RING, GROUP], F32R), sb("hid_l", [P, RING, GROUP], F32R)
        r0 = sb("r0", [P, 2, GROUP])

        flat1 = probs[:, :, :].rearrange("p t s -> p (t s)")[:, 0:2 * GROUP]

        wq0_stage = wide[:, 0, :].rearrange("p (c n) -> p c n", c=DCH)
        wq1_stage = wide[:, 1, :].rearrange("p (c n) -> p c n", c=DCH)
        lora_b = r0[:, :, :].rearrange("p h n -> p (h n)")
        lora_a = hid[:, 0, 0:D]

        side = [ctx.enter_context(nc.psum_tensor(f"side{i}", [P, 512], F32)) for i in range(2)]
        up = [ctx.enter_context(nc.psum_tensor(f"up{i}", [P, 512], F32)) for i in range(2)]
        att_acc = [ctx.enter_context(nc.psum_tensor(f"att_acc{i}", [P, 512], F32)) for i in range(2)]
        ffn_acc = [ctx.enter_context(nc.psum_tensor(f"ffn_acc{i}", [P, 512], F32)) for i in range(2)]

        in_small, in_rope, in_wq0, in_wq1, in_ctxw = sem("in_small"), sem("in_rope"), sem("in_wq0"), sem("in_wq1"), sem("in_ctxw")
        in_outw, in_lora, in_mask1 = sem("in_outw"), sem("in_lora"), sem("in_mask1")
        in_piece = [sem("in_piece0"), sem("in_piece1")]
        piece_hi, piece_lo = sem("piece_hi"), sem("piece_lo")
        prep_dve, prep_act, prep_pool, prep_pe = sem("prep_dve"), sem("prep_act"), sem("prep_pool"), sem("prep_pe")

        GS = (A, B)
        ctx_in, x_in, x_stored = sem("ctx_in"), [sem("x_inA"), sem("x_inB")], [sem("x_stA"), sem("x_stB")]

        def stages(kind):
            return [s for s in PLAN if s[0] == kind]

        norms = [(l, g) for _, l, g in stages("norm")]
        lnT = [(l, g, c) for l, g in norms for c in range(DCH)]
        order_g = {k: [s[1] for s in stages(k)] for k in ("q", "qT", "lg", "soft", "pT", "pv", "res0", "qp", "sc", "out", "res1", "u")}
        side_full = signal("side_full", SIDE)
        acc_full = signal("acc_full", [(s[0], s[1], b) for s in PLAN if s[0] in ("pv", "out") for b in range(2)])
        up_full = signal("up_full", [k for k in CHUNKS])
        delta_full = signal("delta_full", [k for k in CHUNKS if k[0] == 1])
        down_full = signal("down_full", [k for k in CHUNKS])
        xT_hi, xT_lo = signal("xT_hi", lnT), signal("xT_lo", lnT)
        stats, moments, var_ok = signal("stats", norms), signal("moments", norms), signal("var_ok", norms)
        rstd_ok, xn_ok = signal("rstd_ok", norms), signal("xn_ok", norms)
        rot = signal("rot", [(g, h) for g in order_g["q"] for h in range(2)])
        rot_sum = signal("rot_sum", rot.keys)
        qT_hi, qT_lo = signal("qT_hi", rot.keys), signal("qT_lo", rot.keys)
        lg_max = signal("lg_max", [(g, t) for g in order_g["lg"] for t in range(TILES)])
        lg_sub = signal("lg_sub", lg_max.keys)
        exp_ok, sum_ok, inv_ok, prob_ok = (signal(n, [(g,) for g in order_g["soft"]]) for n in ("exp_ok", "sum_ok", "inv_ok", "prob_ok"))
        pT_hi = signal("pT_hi", [(g, k) for g in order_g["pT"] for k in range(3)])
        pT_lo = signal("pT_lo", pT_hi.keys)
        x_att0 = signal("x_att0", [(g, b) for g in order_g["res0"] for b in range(2)])
        x_bias = signal("x_bias", [(g,) for l, g in norms if l == 1])
        qp_ok = signal("qp_ok", [(g, c) for g in order_g["qp"] for c in range(DCH)])
        qp_hi, qp_lo = signal("qp_hi", qp_ok.keys), signal("qp_lo", qp_ok.keys)
        sc_ok, sc_hi, sc_lo = (signal(n, [(g,) for g in order_g["sc"]]) for n in ("sc_ok", "sc_hi", "sc_lo"))
        out_ok = signal("out_ok", [(g, b) for g in order_g["res1"] for b in range(2)])
        x_att1 = signal("x_att1", out_ok.keys)
        u_hi, u_lo = signal("u_hi", [(g,) for g in order_g["u"]]), signal("u_lo", [(g,) for g in order_g["u"]])
        act_ok = signal("act_ok", CHUNKS)
        second = signal("second", [k for k in CHUNKS if k[0] == 1])
        mixed = signal("mixed", [k for k in CHUNKS if k[0] == 1])
        hid_hi0 = signal("hid_hi0", [k for k in CHUNKS if k[0] == 0])
        hid_hi1 = signal("hid_hi1", [k for k in CHUNKS if k[0] == 1])
        hid_lo = signal("hid_lo", CHUNKS)
        x_ffn = signal("x_ffn", [(l, g, b) for l in range(2) for g in GS for b in range(2)])
        c_step = signal("c_step", [(n,) for n in ("stats", "moments", "square", "eps", "mask", "kv", "cos", "sin", "rot")])
        c_rms_ok = signal("c_rms_ok", [()])
        kvT_hi, kvT_lo = signal("kvT_hi", [()]), signal("kvT_lo", [()])
        vo_hi, vo_lo = signal("vo_hi", [(0,), (1,)]), signal("vo_lo", [(0,), (1,)])
        kp_ok, kp_hi, kp_lo = signal("kp_ok", [()]), signal("kp_hi", [()]), signal("kp_lo", [()])
        vp_sum, vp_ok, vp_hi, vp_lo = (signal(n, [()]) for n in ("vp_sum", "vp_ok", "vp_hi", "vp_lo"))

        def freed(tile):
            kind, key = tile[0], tile[1:]
            return {"lnT": (xT_lo, key), "q": (rot, key), "qT": (qT_lo, key), "lg": (lg_sub, key), "pT": (pT_lo, key),
                    "qp": (qp_ok, key), "sc": (sc_ok, key), "u": (u_lo, key), "kv": (c_step, ("kv",)),
                    "kvT": (kvT_lo, ()), "vo": (vo_lo, key), "kp": (kp_ok, ()), "vp": (vp_sum, ())}[kind]

        side_of = {tile: side[n % 2] for n, tile in enumerate(SIDE)}
        slot = {k: n % RING for n, k in enumerate(CHUNKS)}
        before = {k: CHUNKS[n - RING] for n, k in enumerate(CHUNKS) if n >= RING}

        PIECES = [(w_h, w_l, a) for w_h, w_l in ((w1_h, w1_l), (w2_h, w2_l), (wi_h, wi_l), (wo_h, wo_l)) for a in range(2)]

        def half_of(w, a):
            return w[:, a, :] if w.shape[1] == DCH else w[:, a * (FCH // 2):(a + 1) * (FCH // 2), :].rearrange("p c n -> p (c n)")

        block = ctx.enter_context(nc.Block())

        @block.sync
        def _(sp):
            def load_context(i):
                sp.dma_start(ctx_rows[:, :], t_in["ctx"][bass.ds(i, 1), :, :].rearrange("o s d -> (o s) d")).then_inc(ctx_in, 16)
                sp.dma_start(ctx_T[:, :, :], t_in["ctx_T"][bass.ds(i, 1), :, :, :].rearrange("o p c s -> p (o c) s")).then_inc(ctx_in, 16)
                sp.dma_start(mask0[:, :], t_in["mask0"][bass.ds(i, 1), :, :].rearrange("o a s -> (o a) s")).then_inc(ctx_in, 16)

            def load_rows(i, g):
                sp.dma_start(x[:, g, :, :], t_in["x"][bass.ds(i, 1), g, :, :, :].rearrange("o t p d -> p (o t) d")).then_inc(x_in[g], 16)

            def store_rows(i, g):
                sp.dma_start(x_out[bass.ds(i, 1), g, :, :, :].rearrange("o t p d -> p (o t) d"), x[:, g, :, :]).then_inc(x_stored[g], 16)

            load_rows(0, A)
            sp.dma_start(small[:, :], t_in["small"]).then_inc(in_small, 16)
            load_context(0)
            load_rows(0, B)
            with sp.Fori(0, BATCH - 1) as i:
                sp.wait_ge(vp_sum.sem, i + 1)
                load_context(i + 1)
                sp.wait_ge(x_ffn.sem, x_ffn.at(i, 1, A, 1))
                store_rows(i, A)
                sp.wait_ge(x_stored[A], i * 16 + 16)
                load_rows(i + 1, A)
                sp.wait_ge(x_stored[B], i * 16 + 16)
                load_rows(i + 1, B)
            sp.wait_ge(x_ffn.sem, BATCH * len(x_ffn.keys) - 2)
            store_rows(BATCH - 1, A)
            sp.wait_ge(x_stored[A], 16 * BATCH)
            sp.wait_ge(x_stored[B], 16 * BATCH)

        @block.gpsimd
        def _(pool):
            nc.gpsimd.memset(minus_half[:, :], -0.5).then_inc(prep_pool, 1)
            nc.gpsimd.memset(ones3[:, :], 1.0).then_inc(prep_pool, 1)
            nc.gpsimd.memset(kb_h[:, :].bitcast(F32), 0.0).then_inc(prep_pool, 1)
            nc.gpsimd.memset(kb_l[:, :].bitcast(F32), 0.0).then_inc(prep_pool, 1)
            nc.gpsimd.memset(v_pad[:, :, :], 0.0).then_inc(prep_pool, 1)
            nc.gpsimd.memset(probs[:, :, LOGITS:PPAD], 0.0).then_inc(prep_pool, 1)
            pool.wait_ge(prep_pool, 6)
            with pool.Fori(0, BATCH) as i:
                for stage_ in PLAN:
                    kind, key = stage_[0], stage_[1:]
                    if kind == "norm":
                        l, g = key
                        pool.wait_ge(var_ok.sem, var_ok.at(i, l, g))
                        nc.gpsimd.tensor_tensor(rstd[:, :], var[:, :], minus_half[:, :], ALU.pow).then_inc(rstd_ok.sem, 1)
                        if l == 1:
                            pool.wait_ge(xn_ok.sem, xn_ok.at(i, l, g))
                            pool.wait_ge(prep_dve, PREP["gb2"])
                            nc.gpsimd.tensor_tensor(x[:, g, :, :], x[:, g, :, :],
                                                    gb2[:, :].unsqueeze(1).broadcast_to([P, TILES, D]), ALU.add).then_inc(x_bias.sem, 1)
                    elif kind == "kv":
                        pool.wait_ge(c_step.sem, c_step.at(i, "eps"))
                        nc.gpsimd.tensor_tensor(c_rms[:, :], c_sq[:, 1:2], minus_half[0:CTX, 0:1], ALU.pow).then_inc(c_rms_ok.sem, 1)
                    elif kind == "q":
                        g, = key
                        for h in range(2):
                            pool.wait_ge(rot.sem, rot.at(i, g, h))
                            nc.gpsimd.tensor_tensor(xn[:, 2 * h:2 * h + 2, :].rearrange("p t d -> p (t d)"),
                                                    flat1[:, h * 512:(h + 1) * 512], wide[:, h, :], ALU.add).then_inc(rot_sum.sem, 1)
                    elif kind == "qp":
                        g, = key
                        for c in range(DCH):
                            pool.wait_ge(qp_hi.sem, qp_hi.at(i, g, c))
                            nc.gpsimd.tensor_tensor(q_l[:, c, :], flat1[:, c * 512:(c + 1) * 512], q_h[:, c, :].bitcast(F32),
                                                    ALU.subtract).then_inc(qp_lo.sem, 1)
                    elif kind == "res1":
                        g, = key
                        for b in range(2):
                            pool.wait_ge(out_ok.sem, out_ok.at(i, g, b))
                            rows = x[:, g, 2 * b:2 * b + 2, :].rearrange("p t d -> p (t d)")
                            nc.gpsimd.tensor_tensor(rows, rows, wide[:, b, :], ALU.add).then_inc(x_att1.sem, 1)
                    elif kind == "up0" or kind == "delta1":
                        l, (g, c) = int(kind == "delta1"), key
                        s = slot[l, g, c]
                        hi = hid_hi1 if l else hid_hi0
                        pool.wait_ge(hi.sem, hi.at(i, l, g, c))
                        nc.gpsimd.tensor_tensor(hid_l[:, s, :], hid[:, s, :], hid_h[:, s, :].bitcast(F32), ALU.subtract).then_inc(hid_lo.sem, 1)

        @block.scalar
        def _(act):
            act.dma_start(wq0_stage[:, :, :], t_in["wq0"]).then_inc(in_wq0, 16)
            act.dma_start(rope_q[:, :, :, :], t_in["rope_q"]).then_inc(in_rope, 16)
            act.dma_start(rope_k[:, :, :], t_in["rope_k"]).then_inc(in_rope, 16)
            act.dma_start(wkv0[:, :, :], t_in["wkv0"]).then_inc(in_ctxw, 16)
            act.dma_start(wk1[:, :, :], t_in["wk1"]).then_inc(in_ctxw, 16)
            act.dma_start(wv1[:, :, :], t_in["wv1"]).then_inc(in_ctxw, 16)
            act.dma_start(out_w[:, :, :], t_in["out_w"]).then_inc(in_outw, 16)
            act.dma_start(lora_a[:, :], t_in["lora_a"]).then_inc(in_lora, 16)
            act.dma_start(lora_b, t_in["lora_b"]).then_inc(in_lora, 16)
            act.dma_start(topk[:, :], t_in["topk"]).then_inc(in_lora, 16)
            act.dma_start(wq1_stage[:, :, :], t_in["wq1"]).then_inc(in_wq1, 16)
            act.dma_start(mask1[:, :], t_in["mask1"]).then_inc(in_mask1, 16)
            for n in range(2):
                act.dma_start(stage[:, n, :], t_in["pieces"][n]).then_inc(in_piece[n], 16)
            act.wait_ge(in_small, 16)
            nc.scalar.activation(gate[:, :], small[:, C_GATE:C_GATE + 4], ACT.Tanh).then_inc(prep_act, 1)
            for n, (w_h, w_l, a) in enumerate(PIECES):
                act.wait_ge(in_piece[n % 2], 16 * (n // 2 + 1))
                nc.scalar.activation(half_of(w_h, a), stage[:, n % 2, :], ACT.Copy).then_inc(piece_hi, 1)
                if n + 2 < len(PIECES):
                    act.wait_ge(piece_lo, n + 1)
                    act.dma_start(stage[:, n % 2, :], t_in["pieces"][n + 2]).then_inc(in_piece[n % 2], 16)

            with act.Fori(0, BATCH) as i:
                for stage_ in PLAN:
                    kind, key = stage_[0], stage_[1:]
                    if kind == "lnT":
                        l, g = key
                        for c in range(DCH):
                            act.wait_ge(side_full.sem, side_full.at(i, "lnT", l, g, c))
                            nc.scalar.activation(T_h[g][:, c, :], side_of["lnT", l, g, c][:, :], ACT.Copy).then_inc(xT_hi.sem, 1)
                    elif kind == "qT":
                        g, = key
                        for p in range(2):
                            act.wait_ge(side_full.sem, side_full.at(i, "qT", g, p))
                            nc.scalar.activation(q_h[:, p, :], side_of["qT", g, p][:, :], ACT.Copy).then_inc(qT_hi.sem, 1)
                    elif kind == "soft":
                        g, = key
                        act.wait_ge(lg_sub.sem, lg_sub.at(i, g, TILES - 1))
                        nc.scalar.activation(probs[:, :, 0:LOGITS], probs[:, :, 0:LOGITS], ACT.Exp).then_inc(exp_ok.sem, 1)
                    elif kind == "pT":
                        g, = key
                        for k in range(3):
                            act.wait_ge(side_full.sem, side_full.at(i, "pT", g, k))
                            nc.scalar.activation(pT_h(g, k), side_of["pT", g, k][0:PCH, :], ACT.Copy).then_inc(pT_hi.sem, 1)
                    elif kind == "kvT":
                        act.wait_ge(side_full.sem, side_full.at(i, "kvT"))
                        bank = side_of["kvT",]
                        for h in range(2):
                            rows = slice(h * HEAD, (h + 1) * HEAD)
                            nc.scalar.activation(kb_h[rows, h * CTX:(h + 1) * CTX], bank[rows, 0:CTX], ACT.Copy)
                            for p in range(2):
                                at = (2 * p + h) * CTX
                                last = nc.scalar.activation(v_pad[rows, p, at:at + CTX], bank[rows, P:P + CTX], ACT.Copy)
                        last.then_inc(kvT_hi.sem, 1)
                    elif kind == "vo":
                        for n in range(2):
                            cols = 2 - n
                            act.wait_ge(side_full.sem, side_full.at(i, "vo", n))
                            nc.scalar.activation(vo_h[:, 2 * n:2 * n + cols, :].rearrange("p k d -> p (k d)"),
                                                 side_of["vo", n][0:PCH, 0:cols * D], ACT.Copy).then_inc(vo_hi.sem, 1)
                    elif kind == "kp":
                        act.wait_ge(side_full.sem, side_full.at(i, "kp"))
                        act.wait_ge(prep_dve, PREP["bk16"])
                        for c in range(DCH):
                            last = nc.scalar.activation(kp_f[:, c, :], side_of["kp",][:, c * CTX:(c + 1) * CTX], ACT.Relu,
                                                        bias=bk16[:, c:c + 1], scale=1.0 / D ** 0.5)
                        last.then_inc(kp_ok.sem, 1)
                        act.wait_ge(kp_ok.sem, kp_ok.at(i))
                        nc.scalar.activation(kp_h[:, :, :], kp_f[:, :, :], ACT.Copy).then_inc(kp_hi.sem, 1)
                    elif kind == "vp":
                        act.wait_ge(vp_ok.sem, vp_ok.at(i))
                        nc.scalar.activation(vp_h[:, :], vp_f[:, :], ACT.Copy).then_inc(vp_hi.sem, 1)
                    elif kind == "qp":
                        g, = key
                        for c in range(DCH):
                            act.wait_ge(side_full.sem, side_full.at(i, "qp", g, c))
                            nc.scalar.activation(flat1[:, c * 512:(c + 1) * 512], side_of["qp", g, c][:, :], ACT.Relu,
                                                 bias=small[:, C_BQ + c:C_BQ + c + 1]).then_inc(qp_ok.sem, 1)
                            act.wait_ge(qp_ok.sem, qp_ok.at(i, g, c))
                            nc.scalar.activation(q_h[:, c, :], flat1[:, c * 512:(c + 1) * 512], ACT.Copy).then_inc(qp_hi.sem, 1)
                    elif kind == "sc":
                        g, = key
                        act.wait_ge(sc_ok.sem, sc_ok.at(i, g))
                        nc.scalar.activation(T_h[g][0:CTX, 0, :], wide[0:CTX, 0, :], ACT.Copy).then_inc(sc_hi.sem, 1)
                    elif kind == "u":
                        g, = key
                        act.wait_ge(side_full.sem, side_full.at(i, "u", g))
                        nc.scalar.activation(u3[g][:, :], side_of["u", g][0:LORA, :], ACT.Copy).then_inc(u_hi.sem, 1)
                    elif kind == "up0":
                        g, c = key
                        s = slot[0, g, c]
                        act.wait_ge(up_full.sem, up_full.at(i, 0, g, c))
                        if (0, g, c) in before:
                            act.wait_ge(hid_lo.sem, hid_lo.at(i, *before[0, g, c]))
                        nc.scalar.activation(hid[:, s, :], up[c % 2][:, :], ACT.Gelu, bias=small[:, C_B1 + c:C_B1 + c + 1]).then_inc(act_ok.sem, 1)
                    elif kind == "base1":
                        g, c = key
                        act.wait_ge(up_full.sem, up_full.at(i, 1, g, c))
                        if c >= 2 or g == B:
                            prev = (1, g, c - 2) if c >= 2 else (1, A, FCH + c - 2)
                            act.wait_ge(mixed.sem, mixed.at(i, *prev))
                        nc.scalar.activation(r0[:, c % 2, :], up[c % 2][:, :], ACT.Relu).then_inc(act_ok.sem, 1)
                    elif kind == "delta1":
                        g, c = key
                        s = slot[1, g, c]
                        act.wait_ge(mixed.sem, mixed.at(i, 1, g, c))
                        act.wait_ge(down_full.sem, down_full.at(i, *before[1, g, c]))
                        nc.scalar.activation(hid_h[:, s, :], hid[:, s, :], ACT.Copy).then_inc(hid_hi1.sem, 1)
                act.wait_ge(x_ffn.sem, x_ffn.at(i, 1, B, 1))
                act.dma_start(x_out[bass.ds(i, 1), B, :, :, :].rearrange("o t p d -> p (o t) d"), x[:, B, :, :]).then_inc(x_stored[B], 16)

        @block.vector
        def _(dve):
            did = [0]

            def prep(ins, name=None):
                did[0] += 1
                ins.then_inc(prep_dve, 1)
                if name:
                    assert PREP[name] == did[0], (name, did[0])
                dve.wait_ge(prep_dve, did[0])

            v = nc.vector
            dve.wait_ge(in_small, 16)
            prep(v.tensor_scalar(rms1[:, :], small[:, C_RMS:C_RMS + DCH], 1.0, None, ALU.add))
            dve.wait_ge(in_wq0, 16)
            for c in range(DCH):
                prep(v.tensor_scalar(wq0_stage[:, c, :], wq0_stage[:, c, :], rms1[:, c:c + 1], None, ALU.mult))
            prep(v.tensor_copy(wq0_h[:, :, :], wq0_stage[:, :, :]))
            prep(v.tensor_tensor(wq0_l[:, :, :], wq0_stage[:, :, :], wq0_h[:, :, :].bitcast(F32), ALU.subtract), "wq0")
            dve.wait_ge(in_ctxw, 48)
            for c in range(DCH):
                prep(v.tensor_scalar(wkv0[:, c, :], wkv0[:, c, :], rms1[:, c:c + 1], None, ALU.mult))
            prep(v.tensor_scalar(bk16[:, :], small[:, C_BK:C_BK + DCH], 1.0 / D ** 0.5, None, ALU.mult), "bk16")
            dve.wait_ge(prep_act, 1)
            prep(v.tensor_scalar(gb2[:, :], small[:, C_B2:C_B2 + D], gate[:, 2:3], None, ALU.mult), "gb2")
            dve.wait_ge(in_lora, 48)
            prep(v.tensor_scalar(topk16[:, :], topk[:, :], float(RANK), None, ALU.mult))
            lane = small[:, C_LANE:C_LANE + LORA].rearrange("p (b k r) -> p b k r", b=3, k=2)
            hot = [pick[:, n, :].rearrange("p (b k r) -> p b k r", b=3, k=2) for n in range(3)]
            prep(v.memset(pick[:, :, :], 0.0))
            for k in range(2):
                prep(v.tensor_scalar(hot[0][:, :, k, :], lane[:, :, k, :], topk16[:, k:k + 1], None, ALU.is_equal))
            prep(v.tensor_copy(hot[1][:, :, 0, :], hot[0][:, :, 0, :]))
            prep(v.tensor_scalar(hot[2][:, :, 0, :], hot[0][:, :, 0, :], -1.0, None, ALU.mult))
            prep(v.tensor_copy(hot[2][:, :, 1, :], hot[0][:, :, 1, :]), "pick")
            dve.wait_ge(in_wq1, 16)
            prep(v.tensor_copy(wq1_h[:, :, :], wq1_stage[:, :, :]))
            prep(v.tensor_tensor(wq1_l[:, :, :], wq1_stage[:, :, :], wq1_h[:, :, :].bitcast(F32), ALU.subtract), "wq1")
            dve.wait_ge(prep_pe, 1)
            la = up[0][:, 0:DCH * LORA].rearrange("p (c j) -> p c j", c=DCH)
            prep(v.tensor_copy(la_h[:, :, :], la))
            prep(v.tensor_tensor(la_l[:, :, :], la, la_h[:, :, :].bitcast(F32), ALU.subtract), "la")
            for n, (bank2, lb) in enumerate(((side, lb0), (att_acc, lbd))):
                dve.wait_ge(prep_pe, 2 + n)
                for h in range(2):
                    cols = slice(h * 512, (h + 1) * 512)
                    prep(v.tensor_copy(lb[:, cols], bank2[h][0:LORA, :]))
                    low = slice(2 * LORA // 3, LORA)
                    prep(v.tensor_tensor(lb[low, cols], bank2[h][low, :], lb[low, cols].bitcast(F32), ALU.subtract),
                         ("lb0", "lbd")[n] if h else None)
            for n, (w_h, w_l, a) in enumerate(PIECES):
                dve.wait_ge(piece_hi, n + 1)
                v.tensor_tensor(half_of(w_l, a), stage[:, n % 2, :], half_of(w_h, a).bitcast(F32), ALU.subtract).then_inc(piece_lo, 1)

            with dve.Fori(0, BATCH) as i:
                for stage_ in PLAN:
                    kind, key = stage_[0], stage_[1:]
                    if kind == "norm":
                        l, g = key
                        if l == 0:
                            dve.wait_ge(x_in[g], i * 16 + 16)
                        elif l == 1:
                            dve.wait_ge(x_att0.sem, x_att0.at(i, g, 1))
                        elif l == 2:
                            dve.wait_ge(x_ffn.sem, x_ffn.at(i, 0, g, 1))
                        else:
                            dve.wait_ge(x_att1.sem, x_att1.at(i, g, 1))
                        for t in range(TILES):
                            last = v.bn_stats(st[:, t, :], x[:, g, t, :])
                        last.then_inc(stats.sem, 1)
                        dve.drain()
                        for t in range(TILES):
                            last = v.bn_aggr(mv[:, t, :], st[:, t, :])
                        last.then_inc(moments.sem, 1)
                        dve.wait_ge(moments.sem, moments.at(i, l, g))
                        if l == 0:
                            v.tensor_scalar(var[:, :], mv[:, :, 1], 1.0 + RMS_EPS, RMS_EPS * LN_EPS, ALU.mult, ALU.add).then_inc(var_ok.sem, 1)
                        else:
                            v.tensor_scalar(var[:, :], mv[:, :, 1], LN_EPS, None, ALU.add).then_inc(var_ok.sem, 1)
                        dve.wait_ge(rstd_ok.sem, rstd_ok.at(i, l, g))
                        for t in range(TILES):
                            last = v.tensor_scalar(xn[:, t, :], x[:, g, t, :], mv[:, t, 0:1], rstd[:, t:t + 1], ALU.subtract, ALU.mult)
                        last.then_inc(xn_ok.sem, 1)
                    elif kind == "lnT":
                        l, g = key
                        for c in range(DCH):
                            dve.wait_ge(xT_hi.sem, xT_hi.at(i, l, g, c))
                            v.tensor_tensor(T_l[g][:, c, :], side_of["lnT", l, g, c][:, :], T_h[g][:, c, :].bitcast(F32),
                                            ALU.subtract).then_inc(xT_lo.sem, 1)
                    elif kind == "kv":
                        dve.wait_ge(ctx_in, i * 48 + 48)
                        v.bn_stats(c_st[:, :], ctx_rows[:, :]).then_inc(c_step.sem, 1)
                        dve.drain()
                        v.bn_aggr(c_mv[:, :], c_st[:, :]).then_inc(c_step.sem, 1)
                        dve.wait_ge(c_step.sem, c_step.at(i, "moments"))
                        v.scalar_tensor_tensor(c_sq[:, 0:1], c_mv[:, 0:1], c_mv[:, 0:1], c_mv[:, 1:2], ALU.mult, ALU.add).then_inc(c_step.sem, 1)
                        dve.wait_ge(c_step.sem, c_step.at(i, "square"))
                        v.tensor_scalar(c_sq[:, 1:2], c_sq[:, 0:1], RMS_EPS, None, ALU.add).then_inc(c_step.sem, 1)
                        for h in range(HEADS):
                            last = v.tensor_scalar(mask_row[:, h * CTX:(h + 1) * CTX], mask0[:, :], small[0:3, C_FILL:C_FILL + 1],
                                                   small[0:3, C_FILL + 1:C_FILL + 2], ALU.mult, ALU.add)
                        last.then_inc(c_step.sem, 1)
                        dve.wait_ge(side_full.sem, side_full.at(i, "kv"))
                        dve.wait_ge(c_rms_ok.sem, c_rms_ok.at(i))
                        v.tensor_scalar(kv[:, :], side_of["kv",][0:CTX, 0:4 * HEAD], c_rms[:, :], None, ALU.mult).then_inc(c_step.sem, 1)
                        dve.wait_ge(c_step.sem, c_step.at(i, "kv"))
                        v.tensor_tensor(k_cos[:, :], kv[:, 0:2 * HEAD], rope_k[:, 0, :], ALU.mult).then_inc(c_step.sem, 1)
                        quarter = kv[:, 0:2 * HEAD].rearrange("p (h a f) -> p h a f", h=2, a=2)
                        sins = rope_k[:, 1, :].rearrange("p (h a f) -> p h a f", h=2, a=2)
                        rots = k_sin[:, :].rearrange("p (h a f) -> p h a f", h=2, a=2)
                        for a in range(2):
                            last = v.tensor_tensor(rots[:, :, a, :], quarter[:, :, 1 - a, :], sins[:, :, a, :], ALU.mult)
                        last.then_inc(c_step.sem, 1)
                        dve.wait_ge(c_step.sem, c_step.at(i, "sin"))
                        v.tensor_tensor(k_cos[:, :], k_cos[:, :], k_sin[:, :], ALU.add).then_inc(c_step.sem, 1)
                    elif kind == "kvT":
                        dve.wait_ge(kvT_hi.sem, kvT_hi.at(i))
                        for h in range(2):
                            rows, cols = slice(h * HEAD, (h + 1) * HEAD), slice(h * CTX, (h + 1) * CTX)
                            last = v.tensor_tensor(kb_l[rows, cols], side_of["kvT",][rows, 0:CTX], kb_h[rows, cols].bitcast(F32), ALU.subtract)
                        last.then_inc(kvT_lo.sem, 1)
                    elif kind == "vo":
                        for n in range(2):
                            cols = 2 - n
                            dve.wait_ge(vo_hi.sem, vo_hi.at(i, n))
                            v.tensor_tensor(vo_l[:, 2 * n:2 * n + cols, :].rearrange("p k d -> p (k d)"), side_of["vo", n][0:PCH, 0:cols * D],
                                            vo_h[:, 2 * n:2 * n + cols, :].rearrange("p k d -> p (k d)").bitcast(F32), ALU.subtract).then_inc(vo_lo.sem, 1)
                    elif kind == "kp":
                        dve.wait_ge(kp_hi.sem, kp_hi.at(i))
                        v.tensor_tensor(kp_l[:, :, :], kp_f[:, :, :], kp_h[:, :, :].bitcast(F32), ALU.subtract).then_inc(kp_lo.sem, 1)
                    elif kind == "vp":
                        dve.wait_ge(side_full.sem, side_full.at(i, "vp"))
                        v.tensor_tensor(vp_f[:, :], side_of["vp",][0:CTX, 0:D], small[0:CTX, C_BV:C_BV + D], ALU.add).then_inc(vp_sum.sem, 1)
                        dve.wait_ge(vp_sum.sem, vp_sum.at(i))
                        v.tensor_scalar(vp_f[:, :], vp_f[:, :], 0.0, None, ALU.max).then_inc(vp_ok.sem, 1)
                        dve.wait_ge(vp_hi.sem, vp_hi.at(i))
                        v.tensor_tensor(vp_l[:, :], vp_f[:, :], vp_h[:, :].bitcast(F32), ALU.subtract).then_inc(vp_lo.sem, 1)
                    elif kind == "q":
                        g, = key
                        if g == A:
                            dve.wait_ge(in_rope, 32)
                        for h in range(2):
                            dve.wait_ge(side_full.sem, side_full.at(i, "q", g, h))
                            tiles = slice(g * TILES + 2 * h, g * TILES + 2 * h + 2)
                            qs = side_of["q", g, h][:, :].rearrange("p (t h f) -> p t h f", t=2, h=HEADS)
                            cos = flat1[:, h * 512:(h + 1) * 512].rearrange("p (t h f) -> p t h f", t=2, h=HEADS)
                            sin = wide[:, h, :].rearrange("p (t h f) -> p t h f", t=2, h=HEADS)
                            v.tensor_tensor(cos, qs, rope_q[:, tiles, 0, :].unsqueeze(2).broadcast_to([P, 2, HEADS, HEAD]), ALU.mult)
                            for a in range(2):
                                to, fr = slice(a * 32, a * 32 + 32), slice(32 - a * 32, 64 - a * 32)
                                last = v.tensor_tensor(sin[:, :, :, to], qs[:, :, :, fr],
                                                       rope_q[:, tiles, 1, to].unsqueeze(2).broadcast_to([P, 2, HEADS, 32]), ALU.mult)
                            last.then_inc(rot.sem, 1)
                    elif kind == "qT":
                        g, = key
                        for p in range(2):
                            dve.wait_ge(qT_hi.sem, qT_hi.at(i, g, p))
                            v.tensor_tensor(q_l[:, p, :], side_of["qT", g, p][:, :], q_h[:, p, :].bitcast(F32), ALU.subtract).then_inc(qT_lo.sem, 1)
                    elif kind == "lg":
                        g, = key
                        for t in range(TILES):
                            dve.wait_ge(side_full.sem, side_full.at(i, "lg", g, t))
                            lg = side_of["lg", g, t][:, 0:LOGITS].rearrange("p (h s) -> p h s", h=HEADS)
                            v.reduce_max(peak[:, t, :], lg, AX_X).then_inc(lg_max.sem, 1)
                            dve.wait_ge(lg_max.sem, lg_max.at(i, g, t))
                            v.tensor_tensor(probs[:, t, 0:LOGITS].rearrange("p (h s) -> p h s", h=HEADS), lg,
                                            peak[:, t, :].unsqueeze(2).broadcast_to([P, HEADS, CTX]), ALU.subtract).then_inc(lg_sub.sem, 1)
                    elif kind == "soft":
                        g, = key
                        pr = probs[:, :, 0:LOGITS].rearrange("p t (h s) -> p t h s", h=HEADS)
                        dve.wait_ge(exp_ok.sem, exp_ok.at(i, g))
                        v.reduce_sum(total[:, :, :], pr, AX_X).then_inc(sum_ok.sem, 1)
                        dve.wait_ge(sum_ok.sem, sum_ok.at(i, g))
                        v.reciprocal(inv[:, :, :], total[:, :, :]).then_inc(inv_ok.sem, 1)
                        dve.wait_ge(inv_ok.sem, inv_ok.at(i, g))
                        v.tensor_tensor(pr, pr, inv[:, :, :].unsqueeze(3).broadcast_to([P, TILES, HEADS, CTX]), ALU.mult).then_inc(prob_ok.sem, 1)
                    elif kind == "pT":
                        g, = key
                        for k in range(3):
                            dve.wait_ge(pT_hi.sem, pT_hi.at(i, g, k))
                            v.tensor_tensor(pT_l(g, k), side_of["pT", g, k][0:PCH, :], pT_h(g, k).bitcast(F32),
                                            ALU.subtract).then_inc(pT_lo.sem, 1)
                    elif kind == "res0":
                        g, = key
                        for b in range(2):
                            dve.wait_ge(acc_full.sem, acc_full.at(i, "pv", g, b))
                            rows = x[:, g, 2 * b:2 * b + 2, :].rearrange("p t d -> p (t d)")
                            v.scalar_tensor_tensor(rows, att_acc[b][:, :], gate[:, 0:1], rows, ALU.mult, ALU.add).then_inc(x_att0.sem, 1)
                    elif kind == "sc":
                        g, = key
                        if g == A:
                            dve.wait_ge(in_mask1, 16)
                        dve.wait_ge(side_full.sem, side_full.at(i, "sc", g))
                        v.scalar_tensor_tensor(wide[0:CTX, 0, :], side_of["sc", g][0:CTX, :], 0.0, mask1[:, g * GROUP:(g + 1) * GROUP],
                                               ALU.max, ALU.add).then_inc(sc_ok.sem, 1)
                        dve.wait_ge(sc_hi.sem, sc_hi.at(i, g))
                        v.tensor_tensor(T_l[g][0:CTX, 0, :], wide[0:CTX, 0, :], T_h[g][0:CTX, 0, :].bitcast(F32), ALU.subtract).then_inc(sc_lo.sem, 1)
                    elif kind == "res1":
                        g, = key
                        for b in range(2):
                            dve.wait_ge(acc_full.sem, acc_full.at(i, "out", g, b))
                            v.tensor_scalar(wide[:, b, :], att_acc[b][:, :], 0.0, gate[:, 1:2], ALU.max, ALU.mult).then_inc(out_ok.sem, 1)
                    elif kind == "u":
                        g, = key
                        dve.wait_ge(u_hi.sem, u_hi.at(i, g))
                        low = slice(LORA // 3, 2 * LORA // 3)
                        v.tensor_tensor(u3[g][low, :], side_of["u", g][low, :], u3[g][low, :].bitcast(F32), ALU.subtract).then_inc(u_lo.sem, 1)
                    elif kind == "up0":
                        g, c = key
                        s = slot[0, g, c]
                        dve.wait_ge(act_ok.sem, act_ok.at(i, 0, g, c))
                        if (0, g, c) in before:
                            dve.wait_ge(down_full.sem, down_full.at(i, *before[0, g, c]))
                        v.tensor_copy(hid_h[:, s, :], hid[:, s, :]).then_inc(hid_hi0.sem, 1)
                    elif kind == "delta1":
                        g, c = key
                        s = slot[1, g, c]
                        dve.wait_ge(delta_full.sem, delta_full.at(i, 1, g, c))
                        dve.wait_ge(hid_lo.sem, hid_lo.at(i, *before[1, g, c]))
                        v.tensor_scalar(hid[:, s, :], up[c % 2][:, :], 0.0, small[:, C_V + 1:C_V + 2], ALU.max, ALU.mult).then_inc(second.sem, 1)
                        dve.wait_ge(second.sem, second.at(i, 1, g, c))
                        v.scalar_tensor_tensor(hid[:, s, :], r0[:, c % 2, :], small[:, C_V:C_V + 1], hid[:, s, :], ALU.mult, ALU.add).then_inc(mixed.sem, 1)
                    elif kind == "resf":
                        l, g = key
                        dve.wait_ge(down_full.sem, down_full.at(i, l, g, FCH - 1))
                        if l == 0:
                            dve.wait_ge(x_bias.sem, x_bias.at(i, g))
                        for b in range(2):
                            rows = x[:, g, 2 * b:2 * b + 2, :].rearrange("p t d -> p (t d)")
                            v.scalar_tensor_tensor(rows, ffn_acc[b][:, :], gate[:, 2 + l:3 + l], rows, ALU.mult, ALU.add).then_inc(x_ffn.sem, 1)

        @block.tensor
        def _(pe):
            ident = small[:, C_ID:C_ID + P]

            def mm(out, lhsT, rhs, start=False, stop=False):
                return nc.tensor.matmul(out, lhsT, rhs, start=start, stop=stop, skip_group_check=True)

            def split_mm(out, terms, start=True, stop=True):
                n = 3 * len(terms)
                for k, (lh, ll, rh, rl) in enumerate(terms):
                    for m, (a, b) in enumerate(((lh, rh), (lh, rl), (ll, rh))):
                        at = 3 * k + m
                        last = mm(out, a, b, start=start and at == 0, stop=stop and at == n - 1)
                return last

            pe.wait_ge(prep_dve, PREP["pick"])
            for c in range(DCH):
                last = mm(up[0][:, c * LORA:(c + 1) * LORA], lora_a[:, c * P:(c + 1) * P], pick[:, 0, :], start=c == 0, stop=True)
            last.then_inc(prep_pe, 1)
            for n, bank2 in enumerate((side, att_acc)):
                for h in range(2):
                    last = mm(bank2[h][0:LORA, :], pick[:, 1 + n, :], lora_b[:, h * 512:(h + 1) * 512], start=True, stop=True)
                last.then_inc(prep_pe, 1)
            pe.wait_ge(prep_dve, PREP["lbd"])
            pe.wait_ge(prep_pool, 6)

            with pe.Fori(0, BATCH) as i:
                def claim(tile):
                    n = SIDE.index(tile)
                    if n >= 2:
                        sig, k = freed(SIDE[n - 2])
                        pe.wait_ge(sig.sem, sig.at(i, *k))
                    return side_of[tile]

                for stage_ in PLAN:
                    kind, key = stage_[0], stage_[1:]
                    if kind == "lnT":
                        l, g = key
                        pe.wait_ge(xn_ok.sem, xn_ok.at(i, l, g))
                        for c in range(DCH):
                            bank = claim(("lnT", l, g, c))
                            for t in range(TILES):
                                last = nc.tensor.transpose(bank[:, t * P:(t + 1) * P], xn[:, t, c * P:(c + 1) * P], ident)
                            last.then_inc(side_full.sem, 1)
                    elif kind == "kv":
                        pe.wait_ge(ctx_in, i * 48 + 48)
                        bank = claim(("kv",))
                        for c in range(DCH):
                            last = mm(bank[0:CTX, 0:4 * HEAD], ctx_T[:, c, :], wkv0[:, c, :], start=c == 0, stop=c == DCH - 1)
                        last.then_inc(side_full.sem, 1)
                    elif kind == "kvT":
                        pe.wait_ge(c_step.sem, c_step.at(i, "rot"))
                        bank = claim(("kvT",))
                        nc.tensor.transpose(bank[:, 0:CTX], k_cos[:, :], ident[0:CTX, 0:CTX])
                        nc.tensor.transpose(bank[:, P:P + CTX], kv[:, 2 * HEAD:4 * HEAD], ident[0:CTX, 0:CTX]).then_inc(side_full.sem, 1)
                    elif kind == "vo":
                        pe.wait_ge(kvT_hi.sem, kvT_hi.at(i))
                        pe.wait_ge(in_outw, 16)
                        for n in range(2):
                            bank = claim(("vo", n))
                            for m in range(2 - n):
                                k = 2 * n + m
                                pairs = [p for p in range(2) if k * PCH < (p + 1) * PAIR and (k + 1) * PCH > p * PAIR]
                                for p in pairs:
                                    last = mm(bank[0:PCH, m * D:(m + 1) * D], v_pad[:, p, k * PCH:(k + 1) * PCH], out_w[:, p, :],
                                              start=m == 0 and p == pairs[0], stop=p == pairs[-1])
                            last.then_inc(side_full.sem, 1)
                    elif kind == "kp":
                        bank = claim(("kp",))
                        for e in range(DCH):
                            for c in range(DCH):
                                last = mm(bank[:, e * CTX:(e + 1) * CTX], wk1[:, c, e * P:(e + 1) * P], ctx_T[:, c, :],
                                          start=e == 0 and c == 0, stop=c == DCH - 1)
                        last.then_inc(side_full.sem, 1)
                    elif kind == "vp":
                        bank = claim(("vp",))
                        for c in range(DCH):
                            last = mm(bank[0:CTX, 0:D], ctx_T[:, c, :], wv1[:, c, :], start=c == 0, stop=c == DCH - 1)
                        last.then_inc(side_full.sem, 1)
                    elif kind == "q":
                        g, = key
                        pe.wait_ge(xT_lo.sem, xT_lo.at(i, 0, g, DCH - 1))
                        for h in range(2):
                            bank = claim(("q", g, h))
                            for m in range(2):
                                tok = slice((2 * h + m) * P, (2 * h + m + 1) * P)
                                last = split_mm(bank[:, m * D:(m + 1) * D],
                                                [(T_h[g][:, c, tok], T_l[g][:, c, tok], wq0_h[:, c, :], wq0_l[:, c, :]) for c in range(DCH)],
                                                start=m == 0)
                            last.then_inc(side_full.sem, 1)
                    elif kind == "qT":
                        g, = key
                        pe.wait_ge(rot_sum.sem, rot_sum.at(i, g, 1))
                        for p in range(2):
                            bank = claim(("qT", g, p))
                            for t in range(TILES):
                                last = nc.tensor.transpose(bank[:, t * P:(t + 1) * P], xn[:, t, p * P:(p + 1) * P], ident)
                            last.then_inc(side_full.sem, 1)
                    elif kind == "lg":
                        g, = key
                        pe.wait_ge(qT_lo.sem, qT_lo.at(i, g, 1))
                        pe.wait_ge(kvT_lo.sem, kvT_lo.at(i))
                        for t in range(TILES):
                            bank = claim(("lg", g, t))
                            tok = slice(t * P, (t + 1) * P)
                            for p in range(2):
                                split_mm(bank[:, p * PAIR:(p + 1) * PAIR], [(q_h[:, p, tok], q_l[:, p, tok], kb_h[:, :], kb_l[:, :])],
                                         start=p == 0, stop=False)
                            mm(bank[:, 0:LOGITS], ones3[:, :], mask_row[:, :], stop=True).then_inc(side_full.sem, 1)
                    elif kind == "pT":
                        g, = key
                        pe.wait_ge(prob_ok.sem, prob_ok.at(i, g))
                        for k in range(3):
                            bank = claim(("pT", g, k))
                            for t in range(TILES):
                                last = nc.tensor.transpose(bank[0:PCH, t * P:(t + 1) * P], probs[:, t, k * PCH:(k + 1) * PCH], ident)
                            last.then_inc(side_full.sem, 1)
                    elif kind == "pv":
                        g, = key
                        pe.wait_ge(pT_lo.sem, pT_lo.at(i, g, 2))
                        pe.wait_ge(vo_lo.sem, vo_lo.at(i, 1))
                        for t in range(TILES):
                            tok = slice(t * P, (t + 1) * P)
                            last = split_mm(att_acc[t // 2][:, t % 2 * D:(t % 2 + 1) * D],
                                            [(pT_h(g, k)[:, tok], pT_l(g, k)[:, tok], vo_h[:, k, :], vo_l[:, k, :]) for k in range(3)],
                                            start=t % 2 == 0)
                            if t % 2:
                                last.then_inc(acc_full.sem, 1)
                    elif kind == "qp":
                        g, = key
                        pe.wait_ge(xT_lo.sem, xT_lo.at(i, 2, g, DCH - 1))
                        for e in range(DCH):
                            cols = slice(e * P, (e + 1) * P)
                            bank = claim(("qp", g, e))
                            split_mm(bank[:, :], [(wq1_h[:, c, cols], wq1_l[:, c, cols], T_h[g][:, c, :], T_l[g][:, c, :])
                                                  for c in range(DCH)]).then_inc(side_full.sem, 1)
                    elif kind == "sc":
                        g, = key
                        pe.wait_ge(qp_lo.sem, qp_lo.at(i, g, 1))
                        pe.wait_ge(kp_lo.sem, kp_lo.at(i))
                        bank = claim(("sc", g))
                        split_mm(bank[0:CTX, :], [(kp_h[:, c, :], kp_l[:, c, :], q_h[:, c, :], q_l[:, c, :]) for c in range(DCH)]).then_inc(side_full.sem, 1)
                    elif kind == "out":
                        g, = key
                        pe.wait_ge(sc_lo.sem, sc_lo.at(i, g))
                        pe.wait_ge(vp_lo.sem, vp_lo.at(i))
                        for t in range(TILES):
                            tok = slice(t * P, (t + 1) * P)
                            last = split_mm(att_acc[t // 2][:, t % 2 * D:(t % 2 + 1) * D],
                                            [(T_h[g][0:CTX, 0, tok], T_l[g][0:CTX, 0, tok], vp_h[:, :], vp_l[:, :])], start=t % 2 == 0)
                            if t % 2:
                                last.then_inc(acc_full.sem, 1)
                    elif kind == "u":
                        g, = key
                        pe.wait_ge(xT_lo.sem, xT_lo.at(i, 3, g, DCH - 1))
                        bank = claim(("u", g))
                        split_mm(bank[0:LORA, :], [(la_h[:, c, :], la_l[:, c, :], T_h[g][:, c, :], T_l[g][:, c, :]) for c in range(DCH)]).then_inc(side_full.sem, 1)
                    elif kind == "up0" or kind == "base1":
                        l, (g, c) = int(kind == "base1"), key
                        if c == 0:
                            pe.wait_ge(xT_lo.sem, xT_lo.at(i, 2 * l + 1, g, DCH - 1))
                            pe.wait_ge(piece_lo, 6 if l else 2)
                            if l:
                                pe.wait_ge(u_lo.sem, u_lo.at(i, g))
                        n = CHUNKS.index((l, g, c))
                        if n >= 2:
                            prev = CHUNKS[n - 2]
                            sig = second if prev[0] else act_ok
                            pe.wait_ge(sig.sem, sig.at(i, *prev))
                        w_h, w_l = (wi_h, wi_l) if l else (w1_h, w1_l)
                        cols = slice(c * P, (c + 1) * P)
                        last = split_mm(up[c % 2][:, :], [(w_h[:, k, cols], w_l[:, k, cols], T_h[g][:, k, :], T_l[g][:, k, :])
                                                          for k in range(DCH)], stop=not l)
                        if l:
                            last = mm(up[c % 2][:, :], lb0[:, cols], u3[g][:, :], stop=True)
                        last.then_inc(up_full.sem, 1)
                    elif kind == "delta1":
                        g, c = key
                        pe.wait_ge(act_ok.sem, act_ok.at(i, 1, g, c))
                        mm(up[c % 2][:, :], lbd[:, c * P:(c + 1) * P], u3[g][:, :], stop=True).then_inc(delta_full.sem, 1)
                    elif kind == "down":
                        l, g, c = key
                        s = slot[l, g, c]
                        if c == 0:
                            pe.wait_ge(piece_lo, 8 if l else 4)
                            if (l, g) != (0, A):
                                prev = (l, A) if g == B else (0, B)
                                pe.wait_ge(x_ffn.sem, x_ffn.at(i, *prev, 1))
                        pe.wait_ge(hid_lo.sem, hid_lo.at(i, l, g, c))
                        w_h, w_l = (wo_h, wo_l) if l else (w2_h, w2_l)
                        for t in range(TILES):
                            tok = slice(t * P, (t + 1) * P)
                            last = split_mm(ffn_acc[t // 2][:, t % 2 * D:(t % 2 + 1) * D],
                                            [(hid_h[:, s, tok], hid_l[:, s, tok], w_h[:, c, :], w_l[:, c, :])],
                                            start=c == 0 and t % 2 == 0, stop=c == FCH - 1)
                        last.then_inc(down_full.sem, 1)


def _rope(positions, scale):
    freq = (2.0 / HEAD * np.arange(HEAD // 2, dtype=np.float32)).astype(np.float32)
    timescale = np.power(np.float32(10000.0), freq)
    angle = (positions.astype(np.float32)[:, None] / timescale).astype(np.float64)
    cos, sin = np.cos(angle) * scale, np.sin(angle) * scale
    return np.stack([np.concatenate([cos, cos], 1), np.concatenate([-sin, sin], 1)], 1).astype(np.float32)


def _fill_parts():
    parts, left = [], np.float32(MASK_FILL)
    for _ in range(3):
        part = (np.array([left], np.float32).view(np.uint32) & np.uint32(0xFFFF0000)).view(np.float32)[0]
        parts.append(part)
        left = np.float32(left - part)
    return parts


_ORDER = ["small", "x", "ctx", "ctx_T", "mask0", "wq0", "rope_q", "rope_k", "wkv0", "wk1", "wv1", "out_w",
          "lora_a", "lora_b", "topk", "wq1", "mask1", "pieces"]


def kernel(x, ctx_1024, mask_BxS2_bk0, mask_1xSxS2_ff0, g_xattn, g_ffn,
           L0_xattn_rms_scale, L0_xattn_q_w, L0_xattn_kv_w, L0_xattn_out_w,
           L0_ffn_w1, L0_ffn_b1, L0_ffn_w2, L0_ffn_b2,
           L1_xattn_kernel_q, L1_xattn_kernel_k, L1_xattn_kernel_v,
           L1_xattn_bias_q, L1_xattn_bias_k, L1_xattn_bias_v,
           L1_ffn_wi_w, L1_ffn_wo_w, L1_ffn_lora_As, L1_ffn_lora_Bs, L1_ffn_top_k_indices, L1_ffn_top_k_values):
    import concourse.bacc as _bacc
    from concourse.bass_utils import run_bass_kernel_spmd as _run

    def rows(w):
        w = np.asarray(w)
        return w.reshape(-1, P, w.shape[-1]).transpose(1, 0, 2)

    def everywhere(v):
        return np.broadcast_to(np.asarray(v), (P, np.asarray(v).size))

    small = np.zeros((P, C_END), np.float32)
    small[:, C_ID:C_ID + P] = np.eye(P, dtype=np.float32)
    small[:, C_RMS:C_RMS + DCH] = np.asarray(L0_xattn_rms_scale).reshape(DCH, P).T
    small[:, C_B1:C_B1 + FCH] = np.asarray(L0_ffn_b1).reshape(FCH, P).T
    small[:, C_GATE:C_GATE + 2] = everywhere(g_xattn)
    small[:, C_GATE + 2:C_GATE + 4] = everywhere(g_ffn)
    small[:, C_BQ:C_BQ + DCH] = np.asarray(L1_xattn_bias_q).reshape(DCH, P).T
    small[:, C_BK:C_BK + DCH] = np.asarray(L1_xattn_bias_k).reshape(DCH, P).T
    small[:, C_V:C_V + 2] = everywhere(L1_ffn_top_k_values)
    small[:, C_LANE:C_LANE + LORA] = np.arange(P)[:, None] - np.arange(LORA)[None, :] % RANK
    small[:, C_B2:C_B2 + D] = everywhere(L0_ffn_b2)
    small[:, C_BV:C_BV + D] = everywhere(L1_xattn_bias_v)
    for p, part in enumerate(_fill_parts()):
        small[p, C_FILL], small[p, C_FILL + 1] = -part, part

    kv_w = np.asarray(L0_xattn_kv_w)[:, 0]
    ctx = np.asarray(ctx_1024)
    mask0 = np.asarray(mask_BxS2_bk0)
    lora_B = np.asarray(L1_ffn_lora_Bs)
    up_rows = lambda w: np.asarray(w).reshape(2, P, FF)
    down_rows = lambda w: np.asarray(w).reshape(2, FCH // 2, P, D).transpose(0, 2, 1, 3).reshape(2, P, FF)
    arrays = {
        "small": small,
        "x": np.asarray(x).reshape(BATCH, 2, TILES, P, D),
        "ctx": ctx,
        "ctx_T": ctx.transpose(0, 2, 1).reshape(BATCH, DCH, P, CTX).transpose(0, 2, 1, 3),
        "mask0": np.broadcast_to(mask0[:, None, :], (BATCH, 3, CTX)),
        "wq0": rows(np.asarray(L0_xattn_q_w).transpose(1, 0, 2).reshape(D, D)),
        "rope_q": _rope(CTX + np.arange(SEQ), 1.0).reshape(SEQ // P, P, 2, HEAD).transpose(1, 0, 2, 3),
        "rope_k": np.concatenate([_rope(np.arange(CTX), HEAD ** -0.5)] * 2, axis=2),
        "wkv0": rows(np.concatenate([kv_w[0], kv_w[0], kv_w[1], kv_w[1]], axis=1)),
        "wk1": rows(np.asarray(L1_xattn_kernel_k)[0, 0]),
        "wv1": rows(np.asarray(L1_xattn_kernel_v)[0, 0]),
        "out_w": rows(np.asarray(L0_xattn_out_w).reshape(D, D)),
        "lora_a": np.asarray(L1_ffn_lora_As).reshape(EXPERTS * RANK, D),
        "lora_b": lora_B.transpose(0, 2, 1).reshape(EXPERTS * RANK, FF),
        "topk": everywhere(L1_ffn_top_k_indices),
        "wq1": rows(np.asarray(L1_xattn_kernel_q)[0, 0]),
        "mask1": np.asarray(mask_1xSxS2_ff0)[0].T,
        "pieces": np.concatenate([up_rows(L0_ffn_w1), down_rows(L0_ffn_w2),
                                  up_rows(np.asarray(L1_ffn_wi_w).T), down_rows(np.asarray(L1_ffn_wo_w).T)]),
    }
    arrays = {n: np.ascontiguousarray(arrays[n]) for n in _ORDER}

    nc = _bacc.Bacc("TRN2", target_bir_lowering=False, num_devices=1)
    t_in = {n: nc.dram_tensor(f"in_{n}", a.shape, U8 if a.dtype == bool else mybir.dt.from_np(a.dtype), kind="ExternalInput").ap() for n, a in arrays.items()}
    x_out = nc.dram_tensor("out_x", (BATCH, 2, TILES, P, D), F32, kind="ExternalOutput").ap()
    gated_flamingo(nc, t_in, x_out)
    r = _run(nc, [{f"in_{n}": a for n, a in arrays.items()}], core_ids=[0])
    return r.results[0]["out_x"].reshape(BATCH, SEQ, D)
```

```python
from contextlib import ExitStack

import numpy as np

import concourse.bass as bass
from concourse import mybir


F32 = mybir.dt.float32
F32R = mybir.dt.float32r
BF16 = mybir.dt.bfloat16
I32 = mybir.dt.int32
U8 = mybir.dt.uint8
ALU = mybir.AluOpType
ACT = mybir.ActivationFunctionType
AX_X = mybir.AxisListType.X

P = 128
BATCH, SEQ, D = 2, 1024, 256
CTX = 77
HEADS, HEAD = 4, 64
PAIR = 2 * CTX
LOGITS = HEADS * CTX
PCH = -(-LOGITS // 3)
PPAD = 3 * PCH
FF = 1024
FCH = FF // P
DCH = D // P
GROUP = 512
TILES = GROUP // P
A, B = 0, 1
EXPERTS, RANK = 8, 16
LORA = 3 * 2 * RANK
RING = 3
MASK_FILL = -2.3819763e+38
LN_EPS, RMS_EPS = 1e-5, 1e-6

C_ID, C_RMS, C_B1, C_GATE, C_BQ, C_BK, C_V, C_LANE = 0, 128, 130, 138, 142, 144, 146, 148
C_BV = C_LANE + LORA
C_FILL = C_BV + D
C_END = C_FILL + 2
PREP = {"wq0": 5, "wkv0": 7, "bk16": 8, "pick": 15, "gb2": 16, "wq1": 18}
POOL_MEMSETS = 6




def attention0(g):
    return [("stats", 0, g), ("norm", 0, g), ("lnT", 0, g), ("q", g), ("qT", g), ("lg", g, 0), ("lg", g, 1), ("soft", g, 0),
            ("soft", g, 1), ("lg", g, 2), ("lg", g, 3), ("soft", g, 2), ("soft", g, 3), ("pT", g, 0), ("pT", g, 1), ("pv", g, 0),
            ("pT", g, 2), ("pv", g, 1), ("pT", g, 3), ("pv", g, 2), ("pv", g, 3), ("res0", g), ("stats", 1, g), ("norm", 1, g),
            ("lnT", 1, g)]


def attention1(g):
    return [("stats", 2, g), ("norm", 2, g), ("lnT", 2, g), ("qp", g), ("sc", g), ("sc_low", g), ("out", g), ("res1", g),
            ("stats", 3, g), ("norm", 3, g), ("lnT", 3, g), ("u", g)]


def merged(stages, others, places):
    order = []
    for n in range(len(stages) + 1):
        order += [o for o, place in zip(others, places, strict=True) if place == n] + stages[n:n + 1]
    return order


CONTEXT = [("ctx_stats",), ("kv",), ("kvT",), ("vo",), ("kp",), ("vp",), ("vp_low",)]
CONTEXT_AT = [3, 4, 4, 5, 12, 15, 18]
FIRST = merged(attention0(A), CONTEXT, CONTEXT_AT)


LAG = (2, 3)


def feed_forward():
    up, delta, high = [], [], []
    down = {}
    for l in range(2):
        for g in (A, B):
            for c in range(FCH):
                up.append([("base1" if l else "up0", g, c)])
                delta.append([("delta1", g, c)] if l else [("bias", g, c // 2 - 1)] if c in (2, 4) else [])
                high.append([] if l else [("high0", g, c)])
                down[len(up) - 1 + LAG[l]] = [("down", l, g, c)] + ([("resf", l, g)] if c == FCH - 1 else [])
    slots = []
    for u in range(max(down) + 1):
        slots.append(up[u] if u < len(up) else [])
        slots.append(delta[u - 1] if 1 <= u <= len(up) else [])
        slots.append(down.get(u, []) + (high[u] if u < len(up) else []))
    return slots


BESIDE = [
    (attention0(B), 0, [0, 2, 3, 5, 8, 8, 8, 9, 9, 9, 9, 10, 14, 14, 14, 16, 16, 16, 16, 16, 17, 19, 20, 22, 22]),
    (attention1(A), 0, [32, 32, 36, 36, 37, 38, 40, 40, 41, 46, 46, 48]),
    (attention1(B), 0, [55, 56, 58, 60, 63, 63, 65, 66, 66, 68, 70, 71]),
    (FIRST, 1, [73, 75, 75, 75, 76, 76, 78, 81, 82, 82, 82, 82, 83, 84, 84, 86, 86, 86, 86, 88, 89, 89, 89, 89, 90, 90, 90, 90, 90, 90, 92, 95]),
]


FF_SLOTS = feed_forward()
ROW_SLOTS = 2 * 2 * FCH * 3
LOOP_FROM = FCH * 3


def plan(first, last, row):
    order = []
    for n in range(first, last):
        for stages, ahead, slots in BESIDE:
            if row + ahead < BATCH:
                order += [(s, ahead) for s, slot in zip(stages, slots, strict=True) if slot == n]
        if n + ROW_SLOTS < len(FF_SLOTS) and row > 0:
            order += [(s, -1) for s in FF_SLOTS[n + ROW_SLOTS]]
        if n < ROW_SLOTS or row == BATCH - 1:
            order += [(s, 0) for s in FF_SLOTS[n]]
    return order


PREPARE = [("weights",), ("context_weights",), ("picks",), ("lora",), ("query_weights",)]
PREPARE_AT = [2, 4, 4, 6, 21]
PIECES_AT = [4, 10, 12, 15, 19, 23, 28, 30]
PIECES_BESIDE = [0, 4, 8, 11, 11, 17, 22, 23]
PIECE_STAGES = [("piece", n) for n in range(2 * FCH)]
START = [(s, 0) for s in merged(FIRST, PREPARE + PIECE_STAGES[:FCH], PREPARE_AT + PIECES_AT)]
for slot in range(LOOP_FROM):
    START += plan(slot, slot + 1, 0) + [(s, 0) for s, at in zip(PIECE_STAGES[FCH:], PIECES_BESIDE) if at == slot]
BODY = plan(LOOP_FROM, ROW_SLOTS, 0) + [(s, ahead + 1) for s, ahead in plan(0, LOOP_FROM, 1)]
END = plan(LOOP_FROM, len(FF_SLOTS), BATCH - 1)
PLAN = [s for s, _ in START if s[0] not in ("weights", "context_weights", "query_weights", "picks", "lora", "piece")] + [s for s, _ in END]


TILES_OF = {
    "lnT": lambda l, g: [("lnT", l, g, c) for c in range(DCH)],
    "q": lambda g: [("q", g, h) for h in range(2)],
    "qT": lambda g: [("qT", g, p) for p in range(2)],
    "lg": lambda g, t: [("lg", g, t)],
    "pT": lambda g, t: [("pT", g, t)],
    "qp": lambda g: [("qp", g, c) for c in range(DCH)],
    "sc": lambda g: [("sc", g)],
    "u": lambda g: [("u", g)],
    "kv": lambda: [("kv",)],
    "kvT": lambda: [("kvT",)],
    "vo": lambda: [("vo", 0), ("vo", 1)],
    "kp": lambda: [("kp",)],
    "vp": lambda: [("vp",)],
}
SIDE = [t for s in PLAN if s[0] in TILES_OF for t in TILES_OF[s[0]](*s[1:])]
assert len(SIDE) % 2 == 0
CHUNKS = [(l, g, c) for l in range(2) for g in (A, B) for c in range(FCH)]


class Signal:

    def __init__(self, sem, keys):
        self.sem, self.keys = sem, list(keys)
        self.number = {k: n for n, k in enumerate(self.keys)}

    def at(self, i, *key):
        return i * len(self.keys) + (self.number[key] + 1)


def gated_flamingo(nc, t_in, x_out):
    with ExitStack() as ctx:
        def sb(name, shape, dt=F32):
            return ctx.enter_context(nc.sbuf_tensor(name, shape, dt))

        def sem(name):
            return ctx.enter_context(nc.semaphore(name))

        def signal(name, keys):
            return Signal(sem(name), keys)

        small = sb("small", [P, C_END])
        rope_q = sb("rope_q", [P, SEQ // P, 3, HEAD // 2])
        rope_k = sb("rope_k", [CTX, 2, 2 * HEAD])
        wq0_h, wq0_l = sb("wq0_h", [P, DCH, D], F32R), sb("wq0_l", [P, DCH, D], F32R)
        wq1_h, wq1_l = sb("wq1_h", [P, DCH, D], F32R), sb("wq1_l", [P, DCH, D], F32R)
        w1_h, w1_l = sb("w1_h", [P, DCH, FF], F32R), sb("w1_l", [P, DCH, FF], F32R)
        w2_h, w2_l = sb("w2_h", [P, FCH, D], F32R), sb("w2_l", [P, FCH, D], F32R)
        wi_h, wi_l = sb("wi_h", [P, DCH, FF], F32R), sb("wi_l", [P, DCH, FF], F32R)
        wo_h, wo_l = sb("wo_h", [P, FCH, D], F32R), sb("wo_l", [P, FCH, D], F32R)
        wkv0 = sb("wkv0", [P, DCH, 4 * HEAD])
        wk1 = sb("wk1", [P, DCH, D])
        wv1 = sb("wv1", [P, DCH, D])
        out_w = sb("out_w", [P, 2, D])
        mask1 = sb("mask1", [CTX, SEQ])
        la_h, la_l = sb("la_h", [P, DCH, LORA], F32R), sb("la_l", [P, DCH, LORA], F32R)
        lb0 = sb("lb0", [LORA, FF], F32R)
        lbd = sb("lbd", [LORA, FF], F32R)
        rms1 = sb("rms1", [P, DCH])
        gate = sb("gate", [P, 4])
        gb2 = sb("gb2", [P, D])
        bk16 = sb("bk16", [P, DCH])
        minus_half = sb("minus_half", [P, TILES])
        topk = sb("topk", [P, 2], I32)
        topk16 = sb("topk16", [P, 2])
        ones3 = sb("ones3", [3, P], BF16)

        ctx_rows = sb("ctx_rows", [CTX, D])
        ctx_T = sb("ctx_T", [P, DCH, CTX])
        mask0 = sb("mask0", [3, CTX], U8)
        mask_row = sb("mask_row", [3, LOGITS], BF16)
        c_st, c_mv, c_sq, c_rms = sb("c_st", [CTX, 6]), sb("c_mv", [CTX, 2]), sb("c_sq", [CTX, 2]), sb("c_rms", [CTX, 1])
        kv = sb("kv", [CTX, 4 * HEAD])
        k_cos, k_sin = sb("k_cos", [CTX, 2 * HEAD]), sb("k_sin", [CTX, 2 * HEAD])
        kb_h, kb_l = sb("kb_h", [P, PAIR], F32R), sb("kb_l", [P, PAIR], F32R)
        v_pad = sb("v_pad", [P, 2, PPAD])
        vo_h, vo_l = sb("vo_h", [PCH, 3, D], F32R), sb("vo_l", [PCH, 3, D], F32R)
        kp_f = sb("kp_f", [P, DCH, CTX])
        kp_h, kp_l = sb("kp_h", [P, DCH, CTX], F32R), sb("kp_l", [P, DCH, CTX], F32R)
        vp_f = sb("vp_f", [CTX, D])
        vp_h, vp_l = sb("vp_h", [CTX, D], F32R), sb("vp_l", [CTX, D], F32R)

        x = sb("x", [P, 2, TILES, D])
        xn = sb("xn", [P, TILES, D])
        x_raw = sb("x_raw", [P, 2, TILES, D])
        T_h = [sb(f"T_h{g}", [P, 3, GROUP], F32R) for g in (A, B)]
        T_l = [sb(f"T_l{g}", [P, 3, GROUP], F32R) for g in (A, B)]
        q_h, q_l = sb("q_h", [P, 2, GROUP], F32R), sb("q_l", [P, 2, GROUP], F32R)
        probs = sb("probs", [P, TILES, PPAD])
        wide = sb("wide", [P, 2, GROUP])
        st, mv = sb("st", [P, TILES, 6]), sb("mv", [P, TILES, 2])
        var, rstd = sb("var", [P, TILES]), sb("rstd", [P, TILES])
        peak = sb("peak", [P, TILES, HEADS])
        total, inv = sb("total", [P, TILES, HEADS]), sb("inv", [P, TILES, HEADS])
        u3 = [sb(f"u3_{g}", [LORA, GROUP], F32R) for g in (A, B)]
        hid = sb("hid", [P, RING, GROUP])
        hid_h, hid_l = sb("hid_h", [P, RING, GROUP], F32R), sb("hid_l", [P, RING, GROUP], F32R)
        r0 = sb("r0", [P, 2, GROUP])

        flat1 = probs[:, :, :].rearrange("p t s -> p (t s)")[:, 0:2 * GROUP]

        wq0_stage, wq1_stage = x[:, B, 0:2, :], x[:, B, 2:4, :]
        lora_b = x[:, A, :, :].rearrange("p t d -> p (t d)")
        lora_a = x_raw[:, B, 0, :]
        pick = x_raw[:, B, 1:3, :].rearrange("p t d -> p (t d)")[:, 0:3 * LORA].rearrange("p (n j) -> p n j", n=3)
        piece_slots = [hid[:, 0, :], hid[:, 1, :], hid[:, 2, :], r0[:, 0, :], r0[:, 1, :]]
        slot_of_piece = [0, 1, 2, 3, 4, 0, 1, 2] + [3, 4] * 4

        side = [ctx.enter_context(nc.psum_tensor(f"side{i}", [P, 512], F32)) for i in range(2)]
        up = [ctx.enter_context(nc.psum_tensor(f"up{i}", [P, 512], F32)) for i in range(2)]
        att_acc = [ctx.enter_context(nc.psum_tensor(f"att_acc{i}", [P, 512], F32)) for i in range(2)]
        ffn_acc = [ctx.enter_context(nc.psum_tensor(f"ffn_acc{i}", [P, 512], F32)) for i in range(2)]

        lora_psum_a = up[0][:, 0:DCH * LORA].rearrange("p (c j) -> p c j", c=DCH)

        in_wkv, in_rope_k = sem("in_wkv"), sem("in_rope_k")
        in_small, in_rope, in_wq0, in_wq1, in_ctxw = sem("in_small"), sem("in_rope"), sem("in_wq0"), sem("in_wq1"), sem("in_ctxw")
        in_outw, in_lora, in_mask1 = sem("in_outw"), sem("in_lora"), sem("in_mask1")
        in_piece = [sem(f"in_piece{n}") for n in range(5)]
        in_b2 = sem("in_b2")
        piece_hi, piece_lo = sem("piece_hi"), sem("piece_lo")
        gate_ok, lora_hi, lora_lo = sem("gate_ok"), sem("lora_hi"), sem("lora_lo")
        prep_dve, prep_pool, prep_pe = sem("prep_dve"), sem("prep_pool"), sem("prep_pe")

        GS = (A, B)
        ctx_in, x_in, x_free = sem("ctx_in"), [sem("x_inA"), sem("x_inB")], [sem("x_freeA"), sem("x_freeB")]

        def stages(kind):
            return [s for s in PLAN if s[0] == kind]

        norms = [s[1:] for s in stages("norm")]
        lnT = [(l, g, c) for l, g in norms for c in range(DCH)]
        order_g = {k: [s[1] for s in stages(k)] for k in ("q", "qT", "res0", "qp", "sc", "out", "res1", "u")}
        side_full = signal("side_full", SIDE)
        acc_full = signal("acc_full", [key for s in PLAN for key in ([(s[0], s[1], s[2] // 2)] if s[0] == "pv" and s[2] % 2 else
                                                              [("out", s[1], b) for b in range(2)] if s[0] == "out" else [])])
        up_full = signal("up_full", [k for k in CHUNKS])
        delta_full = signal("delta_full", [k for k in CHUNKS if k[0] == 1])
        down_full = signal("down_full", [k for k in CHUNKS])
        xT_hi, xT_lo = signal("xT_hi", lnT), signal("xT_lo", lnT)
        moments, var_ok = signal("moments", norms), signal("var_ok", norms)
        rstd_ok = signal("rstd_ok", norms)
        xn_ok = signal("xn_ok", [(l, g, b) for l, g in norms for b in range(2)])
        rot = signal("rot", [(g, h) for g in order_g["q"] for h in range(2)])
        rot_sum = signal("rot_sum", rot.keys)
        qT_hi, qT_lo = signal("qT_hi", rot.keys), signal("qT_lo", rot.keys)
        lg_min = signal("lg_min", [s[1:] for s in stages("lg")])
        exp_ok, inv_ok = (signal(n, [s[1:] for s in stages("soft")]) for n in ("exp_ok", "inv_ok"))
        prob_ok = signal("prob_ok", exp_ok.keys)
        pT_hi = signal("pT_hi", [s[1:] for s in stages("pT")])
        pT_lo = signal("pT_lo", pT_hi.keys)
        x_att0 = signal("x_att0", [(g, b) for g in order_g["res0"] for b in range(2)])
        x_bias = signal("x_bias", [s[1:] for s in stages("bias")])
        qp_ok = signal("qp_ok", [(g, c) for g in order_g["qp"] for c in range(DCH)])
        qp_hi, qp_lo = signal("qp_hi", qp_ok.keys), signal("qp_lo", qp_ok.keys)
        sc_ok, sc_hi, sc_lo = (signal(n, [(g,) for g in order_g["sc"]]) for n in ("sc_ok", "sc_hi", "sc_lo"))
        out_ok = signal("out_ok", [(g, b) for g in order_g["res1"] for b in range(2)])
        x_att1 = signal("x_att1", out_ok.keys)
        u_hi, u_lo = signal("u_hi", [(g,) for g in order_g["u"]]), signal("u_lo", [(g,) for g in order_g["u"]])
        act_ok = signal("act_ok", CHUNKS)
        second = signal("second", [k for k in CHUNKS if k[0] == 1])
        mixed = signal("mixed", [k for k in CHUNKS if k[0] == 1])
        hid_hi0 = signal("hid_hi0", [k for k in CHUNKS if k[0] == 0])
        hid_hi1 = signal("hid_hi1", [k for k in CHUNKS if k[0] == 1])
        hid_lo = signal("hid_lo", CHUNKS)
        x_ffn = signal("x_ffn", [(l, g, b) for l in range(2) for g in GS for b in range(2)])
        c_step = signal("c_step", [(n,) for n in ("stats", "moments", "square", "eps", "mask", "kv", "cos", "sin", "rot")])
        c_rms_ok = signal("c_rms_ok", [()])
        kvT_hi, kvT_lo = signal("kvT_hi", [()]), signal("kvT_lo", [()])
        vo_hi, vo_lo = signal("vo_hi", [(0,), (1,)]), signal("vo_lo", [(0,), (1,)])
        kp_ok, kp_hi, kp_lo = signal("kp_ok", [()]), signal("kp_hi", [()]), signal("kp_lo", [()])
        vp_sum, vp_ok, vp_hi, vp_lo = (signal(n, [()]) for n in ("vp_sum", "vp_ok", "vp_hi", "vp_lo"))

        def freed(tile):
            kind, key = tile[0], tile[1:]
            return {"lnT": (xT_lo, key), "q": (rot, key), "qT": (qT_lo, key), "lg": (exp_ok, key), "pT": (pT_lo, key),
                    "qp": (qp_ok, key), "sc": (sc_ok, key), "u": (u_lo, key), "kv": (c_step, ("kv",)),
                    "kvT": (kvT_lo, ()), "vo": (vo_lo, key), "kp": (kp_ok, ()), "vp": (vp_sum, ())}[kind]

        side_of = {tile: side[n % 2] for n, tile in enumerate(SIDE)}
        slot = {k: (n + (n >= FCH)) % RING for n, k in enumerate(CHUNKS)}

        def before(i, k, distance=None):
            n = CHUNKS.index(k)
            if distance is None:
                distance = next(d for d in range(1, len(CHUNKS)) if slot[CHUNKS[n - d]] == slot[k])
            if n >= distance:
                return (i,) + CHUNKS[n - distance]
            return None if isinstance(i, int) and i == 0 else (i - 1,) + CHUNKS[n - distance]

        PIECES = [(w_h, w_l, a) for w_h, w_l in ((w1_h, w1_l), (w2_h, w2_l), (wi_h, wi_l), (wo_h, wo_l)) for a in range(4)]

        def piece_of(w, a):
            if w.shape[1] == DCH:
                return w[:, a // 2, a % 2 * 512:(a % 2 + 1) * 512]
            return w[:, 2 * a:2 * a + 2, :].rearrange("p c n -> p (c n)")

        def run(eng, stage):
            for s, _ in START:
                stage(0, *s)
            with eng.Fori(0, BATCH - 1) as i:
                for s, ahead in BODY:
                    stage(i + ahead, *s)
            for s, _ in END:
                stage(BATCH - 1, *s)

        block = ctx.enter_context(nc.Block())

        @block.sync
        def _(sp):
            def load_context(i):
                sp.dma_start(ctx_rows[:, :], t_in["ctx"][bass.ds(i, 1), :, :].rearrange("o s d -> (o s) d")).then_inc(ctx_in, 16)
                sp.dma_start(ctx_T[:, :, :], t_in["ctx_T"][bass.ds(i, 1), :, :, :].rearrange("o p c s -> p (o c) s")).then_inc(ctx_in, 16)
                sp.dma_start(mask0[:, :], t_in["mask0"][bass.ds(i, 1), :, :].rearrange("o a s -> (o a) s")).then_inc(ctx_in, 16)

            def load_rows(i, g):
                sp.dma_start(x_raw[:, g, :, :], t_in["x"][bass.ds(i, 1), g, :, :, :].rearrange("o t p d -> p (o t) d")).then_inc(x_in[g], 16)

            def store_rows(i, g):
                sp.dma_start(x_out[bass.ds(i, 1), g, :, :, :].rearrange("o t p d -> p (o t) d"), x[:, g, :, :]).then_inc(x_free[g], 16)

            sp.sem_inc(x_free[B], 16)
            load_rows(0, A)
            sp.dma_start(small[:, :], t_in["small"]).then_inc(in_small, 16)
            sp.dma_start(wq0_stage, t_in["wq0"]).then_inc(in_wq0, 16)
            load_context(0)
            sp.dma_start(wkv0[:, :, :], t_in["wkv0"]).then_inc(in_wkv, 16)
            sp.dma_start(rope_k[:, :, :], t_in["rope_k"]).then_inc(in_rope_k, 16)
            sp.dma_start(rope_q[:, :, :, :], t_in["rope_q"]).then_inc(in_rope, 16)
            sp.dma_start(out_w[:, :, :], t_in["out_w"]).then_inc(in_outw, 16)
            sp.dma_start(wk1[:, :, :], t_in["wk1"]).then_inc(in_ctxw, 16)
            sp.dma_start(wv1[:, :, :], t_in["wv1"]).then_inc(in_ctxw, 16)
            def load_pieces(first, last):
                for n in range(first, last):
                    k = slot_of_piece[n]
                    if k in slot_of_piece[:n]:
                        sp.wait_ge(piece_lo, n - slot_of_piece[:n][::-1].index(k))
                    sp.dma_start(piece_slots[k], t_in["pieces"][n]).then_inc(in_piece[k], 16)

            load_pieces(0, len(PIECES) // 2)
            sp.wait_ge(prep_pe, 3)
            load_rows(0, B)
            load_pieces(len(PIECES) // 2, len(PIECES))
            sp.dma_start(mask1[:, :], t_in["mask1"]).then_inc(in_mask1, 16)
            with sp.Fori(0, BATCH - 1) as i:
                sp.wait_ge(vp_sum.sem, i + 1)
                load_context(i + 1)
                sp.wait_ge(x_att0.sem, x_att0.at(i, A, 1))
                load_rows(i + 1, A)
                sp.wait_ge(x_att0.sem, x_att0.at(i, B, 1))
                load_rows(i + 1, B)
                for g in (A, B):
                    sp.wait_ge(x_ffn.sem, x_ffn.at(i, 1, g, 1))
                    store_rows(i, g)
            for g in (A, B):
                sp.wait_ge(x_ffn.sem, x_ffn.at(BATCH - 1, 1, g, 1))
                store_rows(BATCH - 1, g)
            sp.wait_ge(x_free[A], 16 * BATCH)
            sp.wait_ge(x_free[B], 16 * BATCH + 16)

        @block.gpsimd
        def _(pool):
            nc.gpsimd.memset(minus_half[:, :], -0.5).then_inc(prep_pool, 1)
            nc.gpsimd.memset(ones3[:, :], 1.0).then_inc(prep_pool, 1)
            nc.gpsimd.memset(kb_h[:, :].bitcast(F32), 0.0).then_inc(prep_pool, 1)
            nc.gpsimd.memset(kb_l[:, :].bitcast(F32), 0.0).then_inc(prep_pool, 1)
            nc.gpsimd.memset(v_pad[:, :, :], 0.0).then_inc(prep_pool, 1)
            nc.gpsimd.memset(probs[:, :, LOGITS:PPAD], 0.0).then_inc(prep_pool, 1)
            pool.wait_ge(prep_pool, POOL_MEMSETS)

            def stage(i, kind, *key):
                if kind == "stats":
                    l, g = key
                    pool.wait_ge(var_ok.sem, var_ok.at(i, l, g))
                    nc.gpsimd.tensor_tensor(rstd[:, :], var[:, :], minus_half[:, :], ALU.pow).then_inc(rstd_ok.sem, 1)
                elif kind == "bias":
                    g, b = key
                    pool.wait_ge(xn_ok.sem, xn_ok.at(i, 1, g, b))
                    pool.wait_ge(prep_dve, PREP["gb2"])
                    rows = x[:, g, 2 * b:2 * b + 2, :]
                    nc.gpsimd.tensor_tensor(rows, rows, gb2[:, :].unsqueeze(1).broadcast_to([P, 2, D]), ALU.add).then_inc(x_bias.sem, 1)
                elif kind == "piece":
                    n, = key
                    w_h, w_l, a = PIECES[n]
                    pool.wait_ge(piece_hi, n + 1)
                    nc.gpsimd.tensor_tensor(piece_of(w_l, a), piece_slots[slot_of_piece[n]], piece_of(w_h, a).bitcast(F32),
                                            ALU.subtract).then_inc(piece_lo, 1)
                elif kind == "soft":
                    g, t = key
                    pool.wait_ge(inv_ok.sem, inv_ok.at(i, g, t))
                    pr = probs[:, t, 0:LOGITS].rearrange("p (h s) -> p h s", h=HEADS)
                    nc.gpsimd.tensor_tensor(pr, pr, inv[:, t, :].unsqueeze(2).broadcast_to([P, HEADS, CTX]), ALU.mult).then_inc(prob_ok.sem, 1)
                elif kind == "ctx_stats":
                    pool.wait_ge(c_step.sem, c_step.at(i, "eps"))
                    nc.gpsimd.tensor_tensor(c_rms[:, :], c_sq[:, 1:2], minus_half[0:CTX, 0:1], ALU.pow).then_inc(c_rms_ok.sem, 1)
                elif kind == "q":
                    g, = key
                    for h in range(2):
                        pool.wait_ge(rot.sem, rot.at(i, g, h))
                        nc.gpsimd.tensor_tensor(xn[:, 2 * h:2 * h + 2, :].rearrange("p t d -> p (t d)"),
                                                flat1[:, h * 512:(h + 1) * 512], wide[:, h, :], ALU.add).then_inc(rot_sum.sem, 1)
                elif kind == "high0" or kind == "delta1":
                    l, (g, c) = int(kind == "delta1"), key
                    s = slot[l, g, c]
                    hi = hid_hi1 if l else hid_hi0
                    pool.wait_ge(hi.sem, hi.at(i, l, g, c))
                    nc.gpsimd.tensor_tensor(hid_l[:, s, :], hid[:, s, :], hid_h[:, s, :].bitcast(F32), ALU.subtract).then_inc(hid_lo.sem, 1)

            run(pool, stage)

        @block.scalar
        def _(act):
            act.dma_start(gb2[:, :], t_in["b2"]).then_inc(in_b2, 16)
            act.dma_start(lora_a, t_in["lora_a"]).then_inc(in_lora, 16)
            act.dma_start(lora_b, t_in["lora_b"]).then_inc(in_lora, 16)
            act.dma_start(topk[:, :], t_in["topk"]).then_inc(in_lora, 16)
            act.dma_start(wq1_stage, t_in["wq1"]).then_inc(in_wq1, 16)

            def stage(i, kind, *key):
                if kind == "weights":
                    act.wait_ge(in_small, 16)
                    nc.scalar.activation(gate[:, :], small[:, C_GATE:C_GATE + 4], ACT.Tanh).then_inc(gate_ok, 1)
                elif kind == "lora":
                    act.wait_ge(prep_pe, 1)
                    nc.scalar.activation(la_h[:, :, :], lora_psum_a, ACT.Copy).then_inc(lora_hi, 1)
                    for n, (banks, lb) in enumerate(((ffn_acc, lb0), (att_acc, lbd))):
                        act.wait_ge(prep_pe, 2 + n)
                        for h in range(2):
                            nc.scalar.activation(lb[:, h * 512:(h + 1) * 512], banks[h][0:LORA, :], ACT.Copy).then_inc(lora_hi, 1)
                elif kind == "piece":
                    n, = key
                    w_h, w_l, a = PIECES[n]
                    act.wait_ge(in_piece[slot_of_piece[n]], 16 * (slot_of_piece[:n].count(slot_of_piece[n]) + 1))
                    nc.scalar.activation(piece_of(w_h, a), piece_slots[slot_of_piece[n]], ACT.Copy).then_inc(piece_hi, 1)
                elif kind == "lnT":
                    l, g = key
                    for c in range(DCH):
                        act.wait_ge(side_full.sem, side_full.at(i, "lnT", l, g, c))
                        nc.scalar.activation(T_h[g][:, c, :], side_of["lnT", l, g, c][:, :], ACT.Copy).then_inc(xT_hi.sem, 1)
                elif kind == "qT":
                    g, = key
                    for p in range(2):
                        act.wait_ge(side_full.sem, side_full.at(i, "qT", g, p))
                        nc.scalar.activation(q_h[:, p, :], side_of["qT", g, p][:, :], ACT.Copy).then_inc(qT_hi.sem, 1)
                elif kind == "lg":
                    g, t = key
                    act.wait_ge(lg_min.sem, lg_min.at(i, g, t))
                    for h in range(HEADS):
                        cols = slice(h * CTX, (h + 1) * CTX)
                        last = nc.scalar.activation(probs[:, t, cols], side_of["lg", g, t][:, cols], ACT.Exp, bias=peak[:, t, h:h + 1],
                                                    scale=-1.0, accum_out=total[:, t, h:h + 1])
                    last.then_inc(exp_ok.sem, 1)
                elif kind == "pT":
                    g, t = key
                    act.wait_ge(side_full.sem, side_full.at(i, "pT", g, t))
                    nc.scalar.activation(T_h[g][0:PCH, :, t * P:(t + 1) * P],
                                         side_of["pT", g, t][0:PCH, 0:3 * P].rearrange("p (k t) -> p k t", k=3), ACT.Copy).then_inc(pT_hi.sem, 1)
                elif kind == "kvT":
                    act.wait_ge(side_full.sem, side_full.at(i, "kvT"))
                    bank = side_of["kvT",]
                    for h in range(2):
                        rows = slice(h * HEAD, (h + 1) * HEAD)
                        nc.scalar.activation(kb_h[rows, h * CTX:(h + 1) * CTX], bank[rows, 0:CTX], ACT.Copy)
                        for p in range(2):
                            at = (2 * p + h) * CTX
                            last = nc.scalar.activation(v_pad[rows, p, at:at + CTX], bank[rows, P:P + CTX], ACT.Copy)
                    last.then_inc(kvT_hi.sem, 1)
                elif kind == "vo":
                    for n in range(2):
                        cols = 2 - n
                        act.wait_ge(side_full.sem, side_full.at(i, "vo", n))
                        nc.scalar.activation(vo_h[:, 2 * n:2 * n + cols, :].rearrange("p k d -> p (k d)"),
                                             side_of["vo", n][0:PCH, 0:cols * D], ACT.Copy).then_inc(vo_hi.sem, 1)
                elif kind == "kp":
                    act.wait_ge(side_full.sem, side_full.at(i, "kp"))
                    act.wait_ge(prep_dve, PREP["bk16"])
                    for c in range(DCH):
                        last = nc.scalar.activation(kp_f[:, c, :], side_of["kp",][:, c * CTX:(c + 1) * CTX], ACT.Relu,
                                                    bias=bk16[:, c:c + 1], scale=1.0 / D ** 0.5)
                    last.then_inc(kp_ok.sem, 1)
                    act.wait_ge(kp_ok.sem, kp_ok.at(i))
                    nc.scalar.activation(kp_h[:, :, :], kp_f[:, :, :], ACT.Copy).then_inc(kp_hi.sem, 1)
                elif kind == "vp":
                    act.wait_ge(vp_ok.sem, vp_ok.at(i))
                    nc.scalar.activation(vp_h[:, :], vp_f[:, :], ACT.Copy).then_inc(vp_hi.sem, 1)
                elif kind == "qp":
                    g, = key
                    for c in range(DCH):
                        act.wait_ge(side_full.sem, side_full.at(i, "qp", g, c))
                        nc.scalar.activation(flat1[:, c * 512:(c + 1) * 512], side_of["qp", g, c][:, :], ACT.Relu,
                                             bias=small[:, C_BQ + c:C_BQ + c + 1]).then_inc(qp_ok.sem, 1)
                        act.wait_ge(qp_ok.sem, qp_ok.at(i, g, c))
                        nc.scalar.activation(q_h[:, c, :], flat1[:, c * 512:(c + 1) * 512], ACT.Copy).then_inc(qp_hi.sem, 1)
                elif kind == "sc":
                    g, = key
                    act.wait_ge(sc_ok.sem, sc_ok.at(i, g))
                    nc.scalar.activation(T_h[g][0:CTX, 0, :], wide[0:CTX, 0, :], ACT.Copy).then_inc(sc_hi.sem, 1)
                elif kind == "res1":
                    g, = key
                    for b in range(2):
                        act.wait_ge(acc_full.sem, acc_full.at(i, "out", g, b))
                        nc.scalar.activation(wide[:, b, :], att_acc[b][:, :], ACT.Relu).then_inc(out_ok.sem, 1)
                elif kind == "u":
                    g, = key
                    act.wait_ge(side_full.sem, side_full.at(i, "u", g))
                    nc.scalar.activation(u3[g][:, :], side_of["u", g][0:LORA, :], ACT.Copy).then_inc(u_hi.sem, 1)
                elif kind == "up0":
                    g, c = key
                    s = slot[0, g, c]
                    act.wait_ge(up_full.sem, up_full.at(i, 0, g, c))
                    held = before(i, (0, g, c))
                    if held:
                        act.wait_ge(hid_lo.sem, hid_lo.at(*held))
                    nc.scalar.activation(hid[:, s, :], up[c % 2][:, :], ACT.Gelu, bias=small[:, C_B1 + c:C_B1 + c + 1]).then_inc(act_ok.sem, 1)
                elif kind == "base1":
                    g, c = key
                    act.wait_ge(up_full.sem, up_full.at(i, 1, g, c))
                    if c >= 2 or g == B:
                        prev = (1, g, c - 2) if c >= 2 else (1, A, FCH + c - 2)
                        act.wait_ge(mixed.sem, mixed.at(i, *prev))
                    nc.scalar.activation(r0[:, c % 2, :], up[c % 2][:, :], ACT.Relu).then_inc(act_ok.sem, 1)
                elif kind == "delta1":
                    g, c = key
                    s = slot[1, g, c]
                    act.wait_ge(mixed.sem, mixed.at(i, 1, g, c))
                    act.wait_ge(down_full.sem, down_full.at(*before(i, (1, g, c))))
                    nc.scalar.activation(hid_h[:, s, :], hid[:, s, :], ACT.Copy).then_inc(hid_hi1.sem, 1)

            run(act, stage)

        @block.vector
        def _(dve):
            did = [0]
            v = nc.vector

            def prep(ins, name=None):
                did[0] += 1
                ins.then_inc(prep_dve, 1)
                if name:
                    assert PREP[name] == did[0], (name, did[0])
                dve.wait_ge(prep_dve, did[0])

            def split(w_h, w_l, w, name):
                prep(v.tensor_copy(w_h, w))
                prep(v.tensor_tensor(w_l, w, w_h.bitcast(F32), ALU.subtract), name)

            def prepare_weights():
                dve.wait_ge(in_small, 16)
                prep(v.tensor_scalar(rms1[:, :], small[:, C_RMS:C_RMS + DCH], 1.0, None, ALU.add))
                dve.wait_ge(in_wq0, 16)
                for c in range(DCH):
                    prep(v.tensor_scalar(wq0_stage[:, c, :], wq0_stage[:, c, :], rms1[:, c:c + 1], None, ALU.mult))
                split(wq0_h[:, :, :], wq0_l[:, :, :], wq0_stage, "wq0")

            def prepare_context_weights():
                dve.wait_ge(in_wkv, 16)
                for c in range(DCH):
                    prep(v.tensor_scalar(wkv0[:, c, :], wkv0[:, c, :], rms1[:, c:c + 1], None, ALU.mult), "wkv0" if c else None)
                prep(v.tensor_scalar(bk16[:, :], small[:, C_BK:C_BK + DCH], 1.0 / D ** 0.5, None, ALU.mult), "bk16")

            def prepare_query_weights():
                dve.wait_ge(gate_ok, 1)
                dve.wait_ge(in_b2, 16)
                prep(v.tensor_scalar(gb2[:, :], gb2[:, :], gate[:, 2:3], None, ALU.mult), "gb2")
                dve.wait_ge(in_wq1, 16)
                split(wq1_h[:, :, :], wq1_l[:, :, :], wq1_stage, "wq1")

            def prepare_lora():
                dve.wait_ge(lora_hi, 1)
                v.tensor_tensor(la_l[:, :, :], lora_psum_a, la_h[:, :, :].bitcast(F32), ALU.subtract).then_inc(lora_lo, 1)
                low = slice(2 * LORA // 3, LORA)
                for n, (banks, lb) in enumerate(((ffn_acc, lb0), (att_acc, lbd))):
                    for h in range(2):
                        cols = slice(h * 512, (h + 1) * 512)
                        dve.wait_ge(lora_hi, 2 + 2 * n + h)
                        v.tensor_tensor(lb[low, cols], banks[h][low, :], lb[low, cols].bitcast(F32), ALU.subtract).then_inc(lora_lo, 1)

            def prepare_picks():
                dve.wait_ge(in_lora, 48)
                prep(v.tensor_scalar(topk16[:, :], topk[:, :], float(RANK), None, ALU.mult))
                lane = small[:, C_LANE:C_LANE + LORA].rearrange("p (b k r) -> p b k r", b=3, k=2)
                hot = [pick[:, n, :].rearrange("p (b k r) -> p b k r", b=3, k=2) for n in range(3)]
                prep(v.memset(pick, 0.0))
                for k in range(2):
                    prep(v.tensor_scalar(hot[0][:, :, k, :], lane[:, :, k, :], topk16[:, k:k + 1], None, ALU.is_equal))
                prep(v.tensor_copy(hot[1][:, :, 0, :], hot[0][:, :, 0, :]))
                prep(v.tensor_scalar(hot[2][:, :, 0, :], hot[0][:, :, 0, :], -1.0, None, ALU.mult))
                prep(v.tensor_copy(hot[2][:, :, 1, :], hot[0][:, :, 1, :]), "pick")

            def stage(i, kind, *key):
                if kind == "weights":
                    prepare_weights()
                elif kind == "picks":
                    prepare_picks()
                elif kind == "lora":
                    prepare_lora()
                elif kind == "context_weights":
                    prepare_context_weights()
                elif kind == "query_weights":
                    prepare_query_weights()
                elif kind == "stats":
                    l, g = key
                    src = x_raw if l == 0 else x
                    for b in range(2):
                        if l == 0 and b == 0:
                            dve.wait_ge(x_in[g], i * 16 + 16)
                        elif l:
                            ready = {1: (x_att0, (g, b)), 2: (x_ffn, (0, g, b)), 3: (x_att1, (g, b))}[l]
                            dve.wait_ge(ready[0].sem, ready[0].at(i, *ready[1]))
                        for t in range(2 * b, 2 * b + 2):
                            last = v.bn_stats(st[:, t, :], src[:, g, t, :])
                    dve.drain()
                    for t in range(TILES):
                        last = v.bn_aggr(mv[:, t, :], st[:, t, :])
                    last.then_inc(moments.sem, 1)
                    dve.wait_ge(moments.sem, moments.at(i, l, g))
                    if l == 0:
                        v.tensor_scalar(var[:, :], mv[:, :, 1], 1.0 + RMS_EPS, RMS_EPS * LN_EPS, ALU.mult, ALU.add).then_inc(var_ok.sem, 1)
                    else:
                        v.tensor_scalar(var[:, :], mv[:, :, 1], LN_EPS, None, ALU.add).then_inc(var_ok.sem, 1)
                elif kind == "norm":
                    l, g = key
                    src = x_raw if l == 0 else x
                    dve.wait_ge(rstd_ok.sem, rstd_ok.at(i, l, g))
                    for t in range(TILES):
                        last = v.tensor_scalar(xn[:, t, :], src[:, g, t, :], mv[:, t, 0:1], rstd[:, t:t + 1], ALU.subtract, ALU.mult)
                        if t % 2:
                            last.then_inc(xn_ok.sem, 1)
                elif kind == "lnT":
                    l, g = key
                    for c in range(DCH):
                        dve.wait_ge(xT_hi.sem, xT_hi.at(i, l, g, c))
                        v.tensor_tensor(T_l[g][:, c, :], side_of["lnT", l, g, c][:, :], T_h[g][:, c, :].bitcast(F32),
                                        ALU.subtract).then_inc(xT_lo.sem, 1)
                elif kind == "ctx_stats":
                    dve.wait_ge(ctx_in, i * 48 + 48)
                    v.bn_stats(c_st[:, :], ctx_rows[:, :]).then_inc(c_step.sem, 1)
                    dve.drain()
                    v.bn_aggr(c_mv[:, :], c_st[:, :]).then_inc(c_step.sem, 1)
                    dve.wait_ge(c_step.sem, c_step.at(i, "moments"))
                    v.scalar_tensor_tensor(c_sq[:, 0:1], c_mv[:, 0:1], c_mv[:, 0:1], c_mv[:, 1:2], ALU.mult, ALU.add).then_inc(c_step.sem, 1)
                    dve.wait_ge(c_step.sem, c_step.at(i, "square"))
                    v.tensor_scalar(c_sq[:, 1:2], c_sq[:, 0:1], RMS_EPS, None, ALU.add).then_inc(c_step.sem, 1)
                    for h in range(HEADS):
                        last = v.tensor_scalar(mask_row[:, h * CTX:(h + 1) * CTX], mask0[:, :], small[0:3, C_FILL:C_FILL + 1],
                                               small[0:3, C_FILL + 1:C_FILL + 2], ALU.mult, ALU.add)
                    last.then_inc(c_step.sem, 1)
                elif kind == "kv":
                    dve.wait_ge(side_full.sem, side_full.at(i, "kv"))
                    dve.wait_ge(c_rms_ok.sem, c_rms_ok.at(i))
                    v.tensor_scalar(kv[:, :], side_of["kv",][0:CTX, 0:4 * HEAD], c_rms[:, :], None, ALU.mult).then_inc(c_step.sem, 1)
                    dve.wait_ge(in_rope_k, 16)
                    dve.wait_ge(c_step.sem, c_step.at(i, "kv"))
                    v.tensor_tensor(k_cos[:, :], kv[:, 0:2 * HEAD], rope_k[:, 0, :], ALU.mult).then_inc(c_step.sem, 1)
                    quarter = kv[:, 0:2 * HEAD].rearrange("p (h a f) -> p h a f", h=2, a=2)
                    sins = rope_k[:, 1, :].rearrange("p (h a f) -> p h a f", h=2, a=2)
                    rots = k_sin[:, :].rearrange("p (h a f) -> p h a f", h=2, a=2)
                    for a in range(2):
                        last = v.tensor_tensor(rots[:, :, a, :], quarter[:, :, 1 - a, :], sins[:, :, a, :], ALU.mult)
                    last.then_inc(c_step.sem, 1)
                    dve.wait_ge(c_step.sem, c_step.at(i, "sin"))
                    v.tensor_tensor(k_cos[:, :], k_cos[:, :], k_sin[:, :], ALU.add).then_inc(c_step.sem, 1)
                elif kind == "kvT":
                    dve.wait_ge(kvT_hi.sem, kvT_hi.at(i))
                    for h in range(2):
                        rows, cols = slice(h * HEAD, (h + 1) * HEAD), slice(h * CTX, (h + 1) * CTX)
                        last = v.tensor_tensor(kb_l[rows, cols], side_of["kvT",][rows, 0:CTX], kb_h[rows, cols].bitcast(F32), ALU.subtract)
                    last.then_inc(kvT_lo.sem, 1)
                elif kind == "vo":
                    for n in range(2):
                        cols = 2 - n
                        dve.wait_ge(vo_hi.sem, vo_hi.at(i, n))
                        v.tensor_tensor(vo_l[:, 2 * n:2 * n + cols, :].rearrange("p k d -> p (k d)"), side_of["vo", n][0:PCH, 0:cols * D],
                                        vo_h[:, 2 * n:2 * n + cols, :].rearrange("p k d -> p (k d)").bitcast(F32), ALU.subtract).then_inc(vo_lo.sem, 1)
                elif kind == "kp":
                    dve.wait_ge(kp_hi.sem, kp_hi.at(i))
                    v.tensor_tensor(kp_l[:, :, :], kp_f[:, :, :], kp_h[:, :, :].bitcast(F32), ALU.subtract).then_inc(kp_lo.sem, 1)
                elif kind == "vp":
                    dve.wait_ge(side_full.sem, side_full.at(i, "vp"))
                    v.tensor_tensor(vp_f[:, :], side_of["vp",][0:CTX, 0:D], small[0:CTX, C_BV:C_BV + D], ALU.add).then_inc(vp_sum.sem, 1)
                    dve.wait_ge(vp_sum.sem, vp_sum.at(i))
                    v.tensor_scalar(vp_f[:, :], vp_f[:, :], 0.0, None, ALU.max).then_inc(vp_ok.sem, 1)
                elif kind == "vp_low":
                    dve.wait_ge(vp_hi.sem, vp_hi.at(i))
                    v.tensor_tensor(vp_l[:, :], vp_f[:, :], vp_h[:, :].bitcast(F32), ALU.subtract).then_inc(vp_lo.sem, 1)
                elif kind == "q":
                    g, = key
                    if g == A:
                        dve.wait_ge(in_rope, 16)
                    for h in range(2):
                        dve.wait_ge(side_full.sem, side_full.at(i, "q", g, h))
                        tiles = slice(g * TILES + 2 * h, g * TILES + 2 * h + 2)
                        qs = side_of["q", g, h][:, :].rearrange("p (t n f) -> p t n f", t=2, f=HEAD // 2)
                        cos = flat1[:, h * 512:(h + 1) * 512].rearrange("p (t n f) -> p t n f", t=2, f=HEAD // 2)
                        sin = wide[:, h, :].rearrange("p (t n f) -> p t n f", t=2, f=HEAD // 2)
                        n = 2 * HEADS
                        v.tensor_tensor(cos, qs, rope_q[:, tiles, 0, :].unsqueeze(2).broadcast_to([P, 2, n, HEAD // 2]), ALU.mult)
                        for a in range(2):
                            last = v.tensor_tensor(sin[:, :, a::2, :], qs[:, :, 1 - a::2, :],
                                                   rope_q[:, tiles, 1 + a, :].unsqueeze(2).broadcast_to([P, 2, HEADS, HEAD // 2]), ALU.mult)
                        last.then_inc(rot.sem, 1)
                elif kind == "qT":
                    g, = key
                    for p in range(2):
                        dve.wait_ge(qT_hi.sem, qT_hi.at(i, g, p))
                        v.tensor_tensor(q_l[:, p, :], side_of["qT", g, p][:, :], q_h[:, p, :].bitcast(F32), ALU.subtract).then_inc(qT_lo.sem, 1)
                elif kind == "lg":
                    g, t = key
                    dve.wait_ge(side_full.sem, side_full.at(i, "lg", g, t))
                    lg = side_of["lg", g, t][:, 0:LOGITS].rearrange("p (h s) -> p h s", h=HEADS)
                    v.tensor_reduce(peak[:, t, :], lg, AX_X, ALU.min).then_inc(lg_min.sem, 1)
                elif kind == "soft":
                    g, t = key
                    dve.wait_ge(exp_ok.sem, exp_ok.at(i, g, t))
                    v.reciprocal(inv[:, t, :], total[:, t, :]).then_inc(inv_ok.sem, 1)
                elif kind == "pT":
                    g, t = key
                    dve.wait_ge(pT_hi.sem, pT_hi.at(i, g, t))
                    cols = slice(t * P, (t + 1) * P)
                    v.tensor_tensor(T_l[g][0:PCH, :, cols], side_of["pT", g, t][0:PCH, 0:3 * P].rearrange("p (k t) -> p k t", k=3),
                                    T_h[g][0:PCH, :, cols].bitcast(F32), ALU.subtract).then_inc(pT_lo.sem, 1)
                elif kind == "res0":
                    g, = key
                    if g == B:
                        dve.wait_ge(x_free[B], i * 16 + 16)
                    elif not (isinstance(i, int) and i == 0):
                        dve.wait_ge(x_free[A], i * 16)
                    for b in range(2):
                        dve.wait_ge(acc_full.sem, acc_full.at(i, "pv", g, b))
                        rows, raw = (w[:, g, 2 * b:2 * b + 2, :].rearrange("p t d -> p (t d)") for w in (x, x_raw))
                        v.scalar_tensor_tensor(rows, att_acc[b][:, :], gate[:, 0:1], raw, ALU.mult, ALU.add).then_inc(x_att0.sem, 1)
                elif kind == "qp":
                    g, = key
                    for c in range(DCH):
                        dve.wait_ge(qp_hi.sem, qp_hi.at(i, g, c))
                        v.tensor_tensor(q_l[:, c, :], flat1[:, c * 512:(c + 1) * 512], q_h[:, c, :].bitcast(F32),
                                        ALU.subtract).then_inc(qp_lo.sem, 1)
                elif kind == "sc":
                    g, = key
                    if g == A:
                        dve.wait_ge(in_mask1, 16)
                    dve.wait_ge(side_full.sem, side_full.at(i, "sc", g))
                    v.scalar_tensor_tensor(wide[0:CTX, 0, :], side_of["sc", g][0:CTX, :], 0.0, mask1[:, g * GROUP:(g + 1) * GROUP],
                                           ALU.max, ALU.add).then_inc(sc_ok.sem, 1)
                elif kind == "sc_low":
                    g, = key
                    dve.wait_ge(sc_hi.sem, sc_hi.at(i, g))
                    v.tensor_tensor(T_l[g][0:CTX, 0, :], wide[0:CTX, 0, :], T_h[g][0:CTX, 0, :].bitcast(F32), ALU.subtract).then_inc(sc_lo.sem, 1)
                elif kind == "res1":
                    g, = key
                    for b in range(2):
                        dve.wait_ge(out_ok.sem, out_ok.at(i, g, b))
                        rows = x[:, g, 2 * b:2 * b + 2, :].rearrange("p t d -> p (t d)")
                        v.scalar_tensor_tensor(rows, wide[:, b, :], gate[:, 1:2], rows, ALU.mult, ALU.add).then_inc(x_att1.sem, 1)
                elif kind == "u":
                    g, = key
                    dve.wait_ge(u_hi.sem, u_hi.at(i, g))
                    low = slice(LORA // 3, 2 * LORA // 3)
                    v.tensor_tensor(u3[g][low, :], side_of["u", g][low, :], u3[g][low, :].bitcast(F32), ALU.subtract).then_inc(u_lo.sem, 1)
                elif kind == "high0":
                    g, c = key
                    s = slot[0, g, c]
                    dve.wait_ge(act_ok.sem, act_ok.at(i, 0, g, c))
                    held = before(i, (0, g, c))
                    if held:
                        dve.wait_ge(down_full.sem, down_full.at(*held))
                    v.tensor_copy(hid_h[:, s, :], hid[:, s, :]).then_inc(hid_hi0.sem, 1)
                elif kind == "delta1":
                    g, c = key
                    s = slot[1, g, c]
                    dve.wait_ge(delta_full.sem, delta_full.at(i, 1, g, c))
                    dve.wait_ge(hid_lo.sem, hid_lo.at(*before(i, (1, g, c))))
                    v.tensor_scalar(hid[:, s, :], up[c % 2][:, :], 0.0, small[:, C_V + 1:C_V + 2], ALU.max, ALU.mult).then_inc(second.sem, 1)
                    dve.wait_ge(second.sem, second.at(i, 1, g, c))
                    v.scalar_tensor_tensor(hid[:, s, :], r0[:, c % 2, :], small[:, C_V:C_V + 1], hid[:, s, :], ALU.mult, ALU.add).then_inc(mixed.sem, 1)
                elif kind == "resf":
                    l, g = key
                    dve.wait_ge(down_full.sem, down_full.at(i, l, g, FCH - 1))
                    if l == 0:
                        dve.wait_ge(x_bias.sem, x_bias.at(i, g, 1))
                    for b in range(2):
                        rows = x[:, g, 2 * b:2 * b + 2, :].rearrange("p t d -> p (t d)")
                        v.scalar_tensor_tensor(rows, ffn_acc[b][:, :], gate[:, 2 + l:3 + l], rows, ALU.mult, ALU.add).then_inc(x_ffn.sem, 1)

            run(dve, stage)

        @block.tensor
        def _(pe):
            ident = small[:, C_ID:C_ID + P]

            def mm(out, lhsT, rhs, start=False, stop=False):
                return nc.tensor.matmul(out, lhsT, rhs, start=start, stop=stop, skip_group_check=True)

            def split_mm(out, terms, start=True, stop=True):
                n = 3 * len(terms)
                for k, (lh, ll, rh, rl) in enumerate(terms):
                    for m, (a, b) in enumerate(((lh, rh), (lh, rl), (ll, rh))):
                        at = 3 * k + m
                        last = mm(out, a, b, start=start and at == 0, stop=stop and at == n - 1)
                return last

            def claim(i, tile):
                n = SIDE.index(tile)
                if n >= 2 or not (isinstance(i, int) and i == 0):
                    sig, k = freed(SIDE[n - 2])
                    pe.wait_ge(sig.sem, sig.at(i if n >= 2 else i - 1, *k))
                return side_of[tile]

            def stage(i, kind, *key):
                if kind == "lora":
                    pe.wait_ge(prep_dve, PREP["pick"])
                    for c in range(DCH):
                        last = mm(up[0][:, c * LORA:(c + 1) * LORA], lora_a[:, c * P:(c + 1) * P], pick[:, 0, :], start=c == 0, stop=True)
                    last.then_inc(prep_pe, 1)
                    for n, banks in enumerate((ffn_acc, att_acc)):
                        for h in range(2):
                            last = mm(banks[h][0:LORA, :], pick[:, 1 + n, :], lora_b[:, h * 512:(h + 1) * 512], start=True, stop=True)
                        last.then_inc(prep_pe, 1)
                elif kind == "lnT":
                    l, g = key
                    if isinstance(i, int) and i == 0:
                        pe.wait_ge(in_small, 16)
                    banks = [claim(i, ("lnT", l, g, c)) for c in range(DCH)]
                    for t in range(TILES):
                        if t % 2 == 0:
                            pe.wait_ge(xn_ok.sem, xn_ok.at(i, l, g, t // 2))
                        for c in range(DCH):
                            last = nc.tensor.transpose(banks[c][:, t * P:(t + 1) * P], xn[:, t, c * P:(c + 1) * P], ident)
                            if t == TILES - 1:
                                last.then_inc(side_full.sem, 1)
                elif kind == "kv":
                    pe.wait_ge(ctx_in, i * 48 + 48)
                    if isinstance(i, int) and i == 0:
                        pe.wait_ge(prep_dve, PREP["wkv0"])
                    bank = claim(i, ("kv",))
                    for c in range(DCH):
                        last = mm(bank[0:CTX, 0:4 * HEAD], ctx_T[:, c, :], wkv0[:, c, :], start=c == 0, stop=c == DCH - 1)
                    last.then_inc(side_full.sem, 1)
                elif kind == "kvT":
                    pe.wait_ge(c_step.sem, c_step.at(i, "rot"))
                    bank = claim(i, ("kvT",))
                    nc.tensor.transpose(bank[:, 0:CTX], k_cos[:, :], ident[0:CTX, 0:CTX])
                    nc.tensor.transpose(bank[:, P:P + CTX], kv[:, 2 * HEAD:4 * HEAD], ident[0:CTX, 0:CTX]).then_inc(side_full.sem, 1)
                elif kind == "vo":
                    pe.wait_ge(kvT_hi.sem, kvT_hi.at(i))
                    pe.wait_ge(in_outw, 16)
                    for n in range(2):
                        bank = claim(i, ("vo", n))
                        for m in range(2 - n):
                            k = 2 * n + m
                            pairs = [p for p in range(2) if k * PCH < (p + 1) * PAIR and (k + 1) * PCH > p * PAIR]
                            for p in pairs:
                                last = mm(bank[0:PCH, m * D:(m + 1) * D], v_pad[:, p, k * PCH:(k + 1) * PCH], out_w[:, p, :],
                                          start=m == 0 and p == pairs[0], stop=p == pairs[-1])
                        last.then_inc(side_full.sem, 1)
                elif kind == "kp":
                    pe.wait_ge(in_ctxw, 32)
                    bank = claim(i, ("kp",))
                    for e in range(DCH):
                        for c in range(DCH):
                            last = mm(bank[:, e * CTX:(e + 1) * CTX], wk1[:, c, e * P:(e + 1) * P], ctx_T[:, c, :],
                                      start=e == 0 and c == 0, stop=c == DCH - 1)
                    last.then_inc(side_full.sem, 1)
                elif kind == "vp":
                    bank = claim(i, ("vp",))
                    for c in range(DCH):
                        last = mm(bank[0:CTX, 0:D], ctx_T[:, c, :], wv1[:, c, :], start=c == 0, stop=c == DCH - 1)
                    last.then_inc(side_full.sem, 1)
                elif kind == "q":
                    g, = key
                    pe.wait_ge(xT_lo.sem, xT_lo.at(i, 0, g, DCH - 1))
                    if isinstance(i, int) and i == 0:
                        pe.wait_ge(prep_dve, PREP["wq0"])
                    for h in range(2):
                        bank = claim(i, ("q", g, h))
                        for m in range(2):
                            tok = slice((2 * h + m) * P, (2 * h + m + 1) * P)
                            last = split_mm(bank[:, m * D:(m + 1) * D],
                                            [(T_h[g][:, c, tok], T_l[g][:, c, tok], wq0_h[:, c, :], wq0_l[:, c, :]) for c in range(DCH)],
                                            start=m == 0)
                        last.then_inc(side_full.sem, 1)
                elif kind == "qT":
                    g, = key
                    pe.wait_ge(rot_sum.sem, rot_sum.at(i, g, 1))
                    for p in range(2):
                        bank = claim(i, ("qT", g, p))
                        for t in range(TILES):
                            last = nc.tensor.transpose(bank[:, t * P:(t + 1) * P], xn[:, t, p * P:(p + 1) * P], ident)
                        last.then_inc(side_full.sem, 1)
                elif kind == "lg":
                    g, t = key
                    pe.wait_ge(qT_lo.sem, qT_lo.at(i, g, 1))
                    pe.wait_ge(kvT_lo.sem, kvT_lo.at(i))
                    pe.wait_ge(prep_pool, POOL_MEMSETS)
                    bank = claim(i, ("lg", g, t))
                    tok = slice(t * P, (t + 1) * P)
                    for p in range(2):
                        split_mm(bank[:, p * PAIR:(p + 1) * PAIR], [(q_h[:, p, tok], q_l[:, p, tok], kb_h[:, :], kb_l[:, :])],
                                 start=p == 0, stop=False)
                    mm(bank[:, 0:LOGITS], ones3[:, :], mask_row[:, :], stop=True).then_inc(side_full.sem, 1)
                elif kind == "pT":
                    g, t = key
                    pe.wait_ge(prob_ok.sem, prob_ok.at(i, g, t))
                    bank = claim(i, ("pT", g, t))
                    for k in range(3):
                        last = nc.tensor.transpose(bank[0:PCH, k * P:(k + 1) * P], probs[:, t, k * PCH:(k + 1) * PCH], ident)
                    last.then_inc(side_full.sem, 1)
                elif kind == "pv":
                    g, t = key
                    pe.wait_ge(pT_lo.sem, pT_lo.at(i, g, t))
                    pe.wait_ge(vo_lo.sem, vo_lo.at(i, 1))
                    if isinstance(i, int) and i == 0:
                        pe.wait_ge(lora_lo, 5)
                    tok = slice(t * P, (t + 1) * P)
                    last = split_mm(att_acc[t // 2][:, t % 2 * D:(t % 2 + 1) * D],
                                    [(T_h[g][0:PCH, k, tok], T_l[g][0:PCH, k, tok], vo_h[:, k, :], vo_l[:, k, :]) for k in range(3)],
                                    start=t % 2 == 0)
                    if t % 2:
                        last.then_inc(acc_full.sem, 1)
                elif kind == "qp":
                    g, = key
                    pe.wait_ge(prep_dve, PREP["wq1"])
                    for e in range(DCH):
                        cols = slice(e * P, (e + 1) * P)
                        bank = claim(i, ("qp", g, e))
                        for c in range(DCH):
                            if e == 0:
                                pe.wait_ge(xT_lo.sem, xT_lo.at(i, 2, g, c))
                            last = split_mm(bank[:, :], [(wq1_h[:, c, cols], wq1_l[:, c, cols], T_h[g][:, c, :], T_l[g][:, c, :])],
                                            start=c == 0, stop=c == DCH - 1)
                        last.then_inc(side_full.sem, 1)
                elif kind == "sc":
                    g, = key
                    pe.wait_ge(qp_lo.sem, qp_lo.at(i, g, 1))
                    pe.wait_ge(kp_lo.sem, kp_lo.at(i))
                    bank = claim(i, ("sc", g))
                    split_mm(bank[0:CTX, :], [(kp_h[:, c, :], kp_l[:, c, :], q_h[:, c, :], q_l[:, c, :]) for c in range(DCH)]).then_inc(side_full.sem, 1)
                elif kind == "out":
                    g, = key
                    pe.wait_ge(sc_lo.sem, sc_lo.at(i, g))
                    pe.wait_ge(vp_lo.sem, vp_lo.at(i))
                    for t in range(TILES):
                        tok = slice(t * P, (t + 1) * P)
                        last = split_mm(att_acc[t // 2][:, t % 2 * D:(t % 2 + 1) * D],
                                        [(T_h[g][0:CTX, 0, tok], T_l[g][0:CTX, 0, tok], vp_h[:, :], vp_l[:, :])], start=t % 2 == 0)
                        if t % 2:
                            last.then_inc(acc_full.sem, 1)
                elif kind == "u":
                    g, = key
                    pe.wait_ge(xT_lo.sem, xT_lo.at(i, 3, g, DCH - 1))
                    bank = claim(i, ("u", g))
                    split_mm(bank[0:LORA, :], [(la_h[:, c, :], la_l[:, c, :], T_h[g][:, c, :], T_l[g][:, c, :]) for c in range(DCH)]).then_inc(side_full.sem, 1)
                elif kind == "up0" or kind == "base1":
                    l, (g, c) = int(kind == "base1"), key
                    if c == 0:
                        pe.wait_ge(piece_lo, len(PIECES) if l else len(PIECES) // 2)
                        pe.wait_ge(lora_lo, 5)
                    prev = before(i, (l, g, c), 2)
                    if prev:
                        sig = second if prev[1] else act_ok
                        pe.wait_ge(sig.sem, sig.at(*prev))
                    w_h, w_l = (wi_h, wi_l) if l else (w1_h, w1_l)
                    cols = slice(c * P, (c + 1) * P)
                    for k in range(DCH):
                        if c == 0:
                            pe.wait_ge(xT_lo.sem, xT_lo.at(i, 2 * l + 1, g, k))
                        last = split_mm(up[c % 2][:, :], [(w_h[:, k, cols], w_l[:, k, cols], T_h[g][:, k, :], T_l[g][:, k, :])],
                                        start=k == 0, stop=not l and k == DCH - 1)
                    if l:
                        if c == 0:
                            pe.wait_ge(u_lo.sem, u_lo.at(i, g))
                        last = mm(up[c % 2][:, :], lb0[:, cols], u3[g][:, :], stop=True)
                    last.then_inc(up_full.sem, 1)
                elif kind == "delta1":
                    g, c = key
                    pe.wait_ge(act_ok.sem, act_ok.at(i, 1, g, c))
                    mm(up[c % 2][:, :], lbd[:, c * P:(c + 1) * P], u3[g][:, :], stop=True).then_inc(delta_full.sem, 1)
                elif kind == "down":
                    l, g, c = key
                    s = slot[l, g, c]
                    if c == 0:
                        prev = before(i, (l, g, c), 1)
                        if prev:
                            pe.wait_ge(x_ffn.sem, x_ffn.at(*prev[:3], 1))
                    pe.wait_ge(hid_lo.sem, hid_lo.at(i, l, g, c))
                    w_h, w_l = (wo_h, wo_l) if l else (w2_h, w2_l)
                    for t in range(TILES):
                        tok = slice(t * P, (t + 1) * P)
                        last = split_mm(ffn_acc[t // 2][:, t % 2 * D:(t % 2 + 1) * D],
                                        [(hid_h[:, s, tok], hid_l[:, s, tok], w_h[:, c, :], w_l[:, c, :])],
                                        start=c == 0 and t % 2 == 0, stop=c == FCH - 1)
                    last.then_inc(down_full.sem, 1)

            run(pe, stage)


def _rope(positions, scale):
    freq = (2.0 / HEAD * np.arange(HEAD // 2, dtype=np.float32)).astype(np.float32)
    timescale = np.power(np.float32(10000.0), freq)
    angle = (positions.astype(np.float32)[:, None] / timescale).astype(np.float64)
    cos, sin = np.cos(angle) * scale, np.sin(angle) * scale
    return np.stack([np.concatenate([cos, cos], 1), np.concatenate([-sin, sin], 1)], 1).astype(np.float32)


def _fill_parts():
    parts, left = [], np.float32(MASK_FILL)
    for _ in range(3):
        part = (np.array([left], np.float32).view(np.uint32) & np.uint32(0xFFFF0000)).view(np.float32)[0]
        parts.append(part)
        left = np.float32(left - part)
    return parts


_ORDER = ["small", "x", "ctx", "ctx_T", "mask0", "wq0", "rope_q", "rope_k", "wkv0", "wk1", "wv1", "out_w",
          "b2", "lora_a", "lora_b", "topk", "wq1", "mask1", "pieces"]


def kernel(x, ctx_1024, mask_BxS2_bk0, mask_1xSxS2_ff0, g_xattn, g_ffn,
           L0_xattn_rms_scale, L0_xattn_q_w, L0_xattn_kv_w, L0_xattn_out_w,
           L0_ffn_w1, L0_ffn_b1, L0_ffn_w2, L0_ffn_b2,
           L1_xattn_kernel_q, L1_xattn_kernel_k, L1_xattn_kernel_v,
           L1_xattn_bias_q, L1_xattn_bias_k, L1_xattn_bias_v,
           L1_ffn_wi_w, L1_ffn_wo_w, L1_ffn_lora_As, L1_ffn_lora_Bs, L1_ffn_top_k_indices, L1_ffn_top_k_values):
    import concourse.bacc as _bacc
    from concourse.bass_utils import run_bass_kernel_spmd as _run

    def rows(w):
        w = np.asarray(w)
        return w.reshape(-1, P, w.shape[-1]).transpose(1, 0, 2)

    def everywhere(v):
        return np.broadcast_to(np.asarray(v), (P, np.asarray(v).size))

    small = np.zeros((P, C_END), np.float32)
    small[:, C_ID:C_ID + P] = np.eye(P, dtype=np.float32)
    small[:, C_RMS:C_RMS + DCH] = np.asarray(L0_xattn_rms_scale).reshape(DCH, P).T
    small[:, C_B1:C_B1 + FCH] = np.asarray(L0_ffn_b1).reshape(FCH, P).T
    small[:, C_GATE:C_GATE + 2] = everywhere(g_xattn)
    small[:, C_GATE + 2:C_GATE + 4] = everywhere(g_ffn)
    small[:, C_BQ:C_BQ + DCH] = np.asarray(L1_xattn_bias_q).reshape(DCH, P).T
    small[:, C_BK:C_BK + DCH] = np.asarray(L1_xattn_bias_k).reshape(DCH, P).T
    small[:, C_V:C_V + 2] = everywhere(L1_ffn_top_k_values)
    small[:, C_LANE:C_LANE + LORA] = np.arange(P)[:, None] - np.arange(LORA)[None, :] % RANK
    small[:, C_BV:C_BV + D] = everywhere(L1_xattn_bias_v)
    for p, part in enumerate(_fill_parts()):
        small[p, C_FILL], small[p, C_FILL + 1] = part, -part

    kv_w = np.asarray(L0_xattn_kv_w)[:, 0]
    ctx = np.asarray(ctx_1024)
    mask0 = np.asarray(mask_BxS2_bk0)
    lora_B = np.asarray(L1_ffn_lora_Bs)
    up_rows = lambda w: np.asarray(w).reshape(DCH, P, 2, 512).transpose(0, 2, 1, 3).reshape(4, P, 512)
    down_rows = lambda w: np.asarray(w).reshape(4, 2, P, D).transpose(0, 2, 1, 3).reshape(4, P, 512)
    arrays = {
        "small": small,
        "x": np.asarray(x).reshape(BATCH, 2, TILES, P, D),
        "ctx": ctx,
        "ctx_T": ctx.transpose(0, 2, 1).reshape(BATCH, DCH, P, CTX).transpose(0, 2, 1, 3),
        "mask0": np.broadcast_to(mask0[:, None, :], (BATCH, 3, CTX)),
        "wq0": rows(np.asarray(L0_xattn_q_w).transpose(1, 0, 2).reshape(D, D)),
        "rope_q": _rope(CTX + np.arange(SEQ), 1.0).reshape(SEQ // P, P, 4, HEAD // 2)[:, :, 1:].transpose(1, 0, 2, 3),
        "rope_k": np.concatenate([_rope(np.arange(CTX), -HEAD ** -0.5)] * 2, axis=2),
        "wkv0": rows(np.concatenate([kv_w[0], kv_w[0], kv_w[1], kv_w[1]], axis=1)),
        "wk1": rows(np.asarray(L1_xattn_kernel_k)[0, 0]),
        "wv1": rows(np.asarray(L1_xattn_kernel_v)[0, 0]),
        "out_w": rows(np.asarray(L0_xattn_out_w).reshape(D, D)),
        "lora_a": np.asarray(L1_ffn_lora_As).reshape(EXPERTS * RANK, D),
        "lora_b": lora_B.transpose(0, 2, 1).reshape(EXPERTS * RANK, FF),
        "topk": everywhere(L1_ffn_top_k_indices),
        "b2": everywhere(L0_ffn_b2),
        "wq1": rows(np.asarray(L1_xattn_kernel_q)[0, 0]),
        "mask1": np.asarray(mask_1xSxS2_ff0)[0].T,
        "pieces": np.concatenate([up_rows(L0_ffn_w1), down_rows(L0_ffn_w2),
                                  up_rows(np.asarray(L1_ffn_wi_w).T), down_rows(np.asarray(L1_ffn_wo_w).T)]),
    }
    arrays = {n: np.ascontiguousarray(arrays[n]) for n in _ORDER}

    nc = _bacc.Bacc("TRN2", target_bir_lowering=False, num_devices=1)
    t_in = {n: nc.dram_tensor(f"in_{n}", a.shape, U8 if a.dtype == bool else mybir.dt.from_np(a.dtype), kind="ExternalInput").ap() for n, a in arrays.items()}
    x_out = nc.dram_tensor("out_x", (BATCH, 2, TILES, P, D), F32, kind="ExternalOutput").ap()
    gated_flamingo(nc, t_in, x_out)
    r = _run(nc, [{f"in_{n}": a for n, a in arrays.items()}], core_ids=[0])
    return r.results[0]["out_x"].reshape(BATCH, SEQ, D)
```
